# Optimizing a Trainium2 kernel written in Bass

```python
import numpy as np
import jax
import jax.numpy as jnp

def _softmax(x, axis=-1):
    return jax.nn.softmax(x, axis=axis)

def _gelu(x):
    return jax.nn.gelu(x, approximate=True)

def _silu(x):
    return jax.nn.silu(x)

def _sigmoid(x):
    return jax.nn.sigmoid(x)

def _layernorm(x, axis=-1, eps=1e-05):
    m = jnp.mean(x, axis=axis, keepdims=True)
    v = jnp.var(x, axis=axis, keepdims=True)
    return (x - m) / jnp.sqrt(v + eps)

def _scatter_add(tgt, idx, src, axis=0):
    return tgt.at[idx].add(src)

def _segment_sum(src, seg, n):
    return jax.ops.segment_sum(src, seg, n)
kernel_name = 'mk_adj_seq_d4_adj_r2_ac4776'

def setup_inputs(seed: int=0):
    np.random.seed(seed)
    _w = jnp.asarray

    def _rec_inputs():
        import jax
        import jax.numpy as jnp
        _gk = jax.random.key(seed)
        x = -0.0005207 + 1.001 * jax.random.normal(jax.random.fold_in(_gk, 1), (8, 1024, 256), jnp.float32)
        _a = jax.random.bernoulli(jax.random.fold_in(_gk, 2), 0.00390625, (8, 1024, 1024))
        _a = jnp.logical_or(_a, jnp.swapaxes(_a, -1, -2))
        _a = jnp.logical_or(_a, jnp.eye(1024, dtype=bool))
        _af = _a.astype(jnp.float32)
        _af = _af * jax.random.uniform(jax.random.fold_in(_gk, 3), (8, 1024, 1024), jnp.float32, 0.05, 1)
        adj = _af
        return (x, adj)
    x, adj = _rec_inputs()

    def _L0_gnn_setup():
        import jax, jax.numpy as jnp
        import numpy as np
        NUM_HEADS = 8
        EPS = 1e-09
        key = jax.random.key(seed)
        ks = jax.random.split(key, 8)
        B, N, D = (2, 1024, 256)
        s = 1.0 / np.sqrt(D)
        x = jax.random.normal(ks[0], (B, N, D), dtype=jnp.float32)
        adjacency = jax.random.uniform(ks[1], (B, N, N), dtype=jnp.float32)
        W_q = jax.random.normal(ks[2], (D, D), dtype=jnp.float32) * s
        W_k = jax.random.normal(ks[3], (D, D), dtype=jnp.float32) * s
        W_v = jax.random.normal(ks[4], (D, D), dtype=jnp.float32) * s
        b_q = jnp.zeros((D,), jnp.float32)
        b_k = jnp.zeros((D,), jnp.float32)
        b_v = jnp.zeros((D,), jnp.float32)
        w_g = jax.random.normal(ks[5], (2 * D,), dtype=jnp.float32) * (1.0 / np.sqrt(2 * D))
        b_g = jnp.zeros((), jnp.float32)
        return {'x': x, 'adjacency': adjacency, 'W_q': W_q, 'b_q': b_q, 'W_k': W_k, 'b_k': b_k, 'W_v': W_v, 'b_v': b_v, 'w_g': w_g, 'b_g': b_g}
    _L0_gnn_all = _L0_gnn_setup()
    _L0_gnn_in = {k: v for k, v in _L0_gnn_all.items() if k in ('W_q', 'b_q', 'W_k', 'b_k', 'W_v', 'b_v', 'w_g', 'b_g')}
    del _L0_gnn_all

    def _L1_gnn_setup():
        import jax, jax.numpy as jnp
        import numpy as np
        BS, N, H = (8, 1024, 256)
        NEG_INF = -1000000000.0
        LEAKY_SLOPE = 0.01
        key = jax.random.key(seed)
        ks = jax.random.split(key, 8)
        feats = jax.random.normal(ks[0], (BS, N, H), dtype=jnp.float32)
        adj = jax.random.randint(ks[1], (BS, N, N), 0, 2).astype(jnp.float32)
        adj = jnp.maximum(adj, jnp.eye(N, dtype=jnp.float32)[None])
        s = 1.0 / np.sqrt(H)
        return {'feats': feats, 'adj_mat': adj, 'fc_w': jax.random.normal(ks[2], (H, H), dtype=jnp.float32) * s, 'fc_b': jax.random.normal(ks[3], (H,), dtype=jnp.float32) * s, 'q_w': jax.random.normal(ks[4], (1, H), dtype=jnp.float32) * s, 'q_b': jax.random.normal(ks[5], (1,), dtype=jnp.float32) * s, 'k_w': jax.random.normal(ks[6], (1, H), dtype=jnp.float32) * s, 'k_b': jax.random.normal(ks[7], (1,), dtype=jnp.float32) * s}
    _L1_gnn_all = _L1_gnn_setup()
    _L1_gnn_in = {k: v for k, v in _L1_gnn_all.items() if k in ('fc_w', 'fc_b', 'q_w', 'q_b', 'k_w', 'k_b')}
    del _L1_gnn_all

    def _L2_gnn_setup():
        import jax, jax.numpy as jnp
        import numpy as np
        import math
        D_MODEL = 256
        NHEAD = 8
        HEAD_DIM = D_MODEL // NHEAD
        LN_EPS = 1e-05

        def _layernorm(x, g, b):
            mu = jnp.mean(x, axis=-1, keepdims=True)
            var = jnp.mean(jnp.square(x - mu), axis=-1, keepdims=True)
            return (x - mu) * jax.lax.rsqrt(var + LN_EPS) * g + b
        key = jax.random.key(seed)
        ks = jax.random.split(key, 12)
        B, N, D = (4, 1024, D_MODEL)
        s = 1.0 / math.sqrt(D)
        inp = {'hidden': jax.random.normal(ks[0], (B, N, D), jnp.float32), 'adjacency': (jax.random.uniform(ks[1], (B, N, N)) > 0.98).astype(jnp.float32), 'Wq': jax.random.normal(ks[2], (D, D), jnp.float32) * s, 'bq': jnp.zeros((D,), jnp.float32), 'Wk': jax.random.normal(ks[3], (D, D), jnp.float32) * s, 'bk': jnp.zeros((D,), jnp.float32), 'Wv': jax.random.normal(ks[4], (D, D), jnp.float32) * s, 'bv': jnp.zeros((D,), jnp.float32), 'Wo': jax.random.normal(ks[5], (D, D), jnp.float32) * s, 'bo': jnp.zeros((D,), jnp.float32), 'g1': jnp.ones((D,), jnp.float32), 'b1': jnp.zeros((D,), jnp.float32), 'g2': jnp.ones((D,), jnp.float32), 'b2': jnp.zeros((D,), jnp.float32), 'Wf1': jax.random.normal(ks[6], (D, 4 * D), jnp.float32) * s, 'bf1': jnp.zeros((4 * D,), jnp.float32), 'Wf2': jax.random.normal(ks[7], (4 * D, D), jnp.float32) * (1.0 / math.sqrt(4 * D)), 'bf2': jnp.zeros((D,), jnp.float32)}
        return inp
    _L2_gnn_all = _L2_gnn_setup()
    _L2_gnn_in = {k: v for k, v in _L2_gnn_all.items() if k in ('Wq', 'bq', 'Wk', 'bk', 'Wv', 'bv', 'Wo', 'bo', 'g1', 'b1', 'g2', 'b2', 'Wf1', 'bf1', 'Wf2', 'bf2')}
    del _L2_gnn_all

    def _L3_gnn_setup():
        import jax, jax.numpy as jnp
        import numpy as np
        B, N, D, H = (8, 512, 256, 8)
        DK = D // H
        LN_EPS = 1e-05
        ADJ_MIN = 1e-08

        def _layer_norm(x, gamma, beta):
            mu = jnp.mean(x, axis=-1, keepdims=True)
            var = jnp.mean(jnp.square(x - mu), axis=-1, keepdims=True)
            return (x - mu) * jax.lax.rsqrt(var + LN_EPS) * gamma + beta
        key = jax.random.key(seed)
        ks = jax.random.split(key, 12)
        x = jax.random.normal(ks[0], (B, N, D), dtype=jnp.float32)
        adj = jax.random.uniform(ks[1], (B, N, N), dtype=jnp.float32)
        adj = adj / jnp.sum(adj, axis=-1, keepdims=True)
        s = 1.0 / np.sqrt(D)
        Wq = jax.random.normal(ks[2], (D, D), dtype=jnp.float32) * s
        bq = jnp.zeros((D,), dtype=jnp.float32)
        Wk = jax.random.normal(ks[3], (D, D), dtype=jnp.float32) * s
        bk = jnp.zeros((D,), dtype=jnp.float32)
        Wv = jax.random.normal(ks[4], (D, D), dtype=jnp.float32) * s
        bv = jnp.zeros((D,), dtype=jnp.float32)
        Wo = jax.random.normal(ks[5], (D, D), dtype=jnp.float32) * s
        bo = jnp.zeros((D,), dtype=jnp.float32)
        gamma = jnp.ones((D,), dtype=jnp.float32)
        beta = jnp.zeros((D,), dtype=jnp.float32)
        return {'x': x, 'adj': adj, 'Wq': Wq, 'bq': bq, 'Wk': Wk, 'bk': bk, 'Wv': Wv, 'bv': bv, 'Wo': Wo, 'bo': bo, 'gamma': gamma, 'beta': beta}
    _L3_gnn_all = _L3_gnn_setup()
    _L3_gnn_in = {k: v for k, v in _L3_gnn_all.items() if k in ('Wq', 'bq', 'Wk', 'bk', 'Wv', 'bv', 'Wo', 'bo', 'gamma', 'beta')}
    del _L3_gnn_all
    return {'x': x, 'adj': adj, 'L0_gnn_W_q': _L0_gnn_in['W_q'], 'L0_gnn_b_q': _L0_gnn_in['b_q'], 'L0_gnn_W_k': _L0_gnn_in['W_k'], 'L0_gnn_b_k': _L0_gnn_in['b_k'], 'L0_gnn_W_v': _L0_gnn_in['W_v'], 'L0_gnn_b_v': _L0_gnn_in['b_v'], 'L0_gnn_w_g': _L0_gnn_in['w_g'], 'L0_gnn_b_g': _L0_gnn_in['b_g'], 'L1_gnn_fc_w': _L1_gnn_in['fc_w'], 'L1_gnn_fc_b': _L1_gnn_in['fc_b'], 'L1_gnn_q_w': _L1_gnn_in['q_w'], 'L1_gnn_q_b': _L1_gnn_in['q_b'], 'L1_gnn_k_w': _L1_gnn_in['k_w'], 'L1_gnn_k_b': _L1_gnn_in['k_b'], 'L2_gnn_Wq': _L2_gnn_in['Wq'], 'L2_gnn_bq': _L2_gnn_in['bq'], 'L2_gnn_Wk': _L2_gnn_in['Wk'], 'L2_gnn_bk': _L2_gnn_in['bk'], 'L2_gnn_Wv': _L2_gnn_in['Wv'], 'L2_gnn_bv': _L2_gnn_in['bv'], 'L2_gnn_Wo': _L2_gnn_in['Wo'], 'L2_gnn_bo': _L2_gnn_in['bo'], 'L2_gnn_g1': _L2_gnn_in['g1'], 'L2_gnn_b1': _L2_gnn_in['b1'], 'L2_gnn_g2': _L2_gnn_in['g2'], 'L2_gnn_b2': _L2_gnn_in['b2'], 'L2_gnn_Wf1': _L2_gnn_in['Wf1'], 'L2_gnn_bf1': _L2_gnn_in['bf1'], 'L2_gnn_Wf2': _L2_gnn_in['Wf2'], 'L2_gnn_bf2': _L2_gnn_in['bf2'], 'L3_gnn_Wq': _L3_gnn_in['Wq'], 'L3_gnn_bq': _L3_gnn_in['bq'], 'L3_gnn_Wk': _L3_gnn_in['Wk'], 'L3_gnn_bk': _L3_gnn_in['bk'], 'L3_gnn_Wv': _L3_gnn_in['Wv'], 'L3_gnn_bv': _L3_gnn_in['bv'], 'L3_gnn_Wo': _L3_gnn_in['Wo'], 'L3_gnn_bo': _L3_gnn_in['bo'], 'L3_gnn_gamma': _L3_gnn_in['gamma'], 'L3_gnn_beta': _L3_gnn_in['beta']}

def reference(x, adj, L0_gnn_W_q, L0_gnn_b_q, L0_gnn_W_k, L0_gnn_b_k, L0_gnn_W_v, L0_gnn_b_v, L0_gnn_w_g, L0_gnn_b_g, L1_gnn_fc_w, L1_gnn_fc_b, L1_gnn_q_w, L1_gnn_q_b, L1_gnn_k_w, L1_gnn_k_b, L2_gnn_Wq, L2_gnn_bq, L2_gnn_Wk, L2_gnn_bk, L2_gnn_Wv, L2_gnn_bv, L2_gnn_Wo, L2_gnn_bo, L2_gnn_g1, L2_gnn_b1, L2_gnn_g2, L2_gnn_b2, L2_gnn_Wf1, L2_gnn_bf1, L2_gnn_Wf2, L2_gnn_bf2, L3_gnn_Wq, L3_gnn_bq, L3_gnn_Wk, L3_gnn_bk, L3_gnn_Wv, L3_gnn_bv, L3_gnn_Wo, L3_gnn_bo, L3_gnn_gamma, L3_gnn_beta):
    import jax
    import jax.numpy as jnp

    def _L0_gnn_ref(x, adjacency, W_q, b_q, W_k, b_k, W_v, b_v, w_g, b_g):
        import jax, jax.numpy as jnp
        import numpy as np
        NUM_HEADS = 8
        EPS = 1e-09
        B, N, D = x.shape
        H = NUM_HEADS
        hd = D // H
        Q = (x @ W_q + b_q).reshape(B, N, H, hd)
        K = (x @ W_k + b_k).reshape(B, N, H, hd)
        V = (x @ W_v + b_v).reshape(B, N, H, hd)
        scores = jnp.einsum('bihd,bjhd->bhij', Q, K) / jnp.sqrt(jnp.float32(hd))
        a = x @ w_g[:D]
        c = x @ w_g[D:]
        soul_bias = a[:, :, None] + c[:, None, :] + b_g
        scores = scores + (soul_bias + jnp.log(adjacency + EPS))[:, None, :, :]
        attn = jax.nn.softmax(scores, axis=-1)
        out = jnp.einsum('bhij,bjhd->bihd', attn, V).reshape(B, N, D)
        return out + x

    def _L1_gnn_ref(feats, adj_mat, fc_w, fc_b, q_w, q_b, k_w, k_b):
        import jax, jax.numpy as jnp
        import numpy as np
        BS, N, H = (8, 1024, 256)
        NEG_INF = -1000000000.0
        LEAKY_SLOPE = 0.01
        feat_proj = jnp.einsum('bnh,oh->bno', feats, fc_w) + fc_b
        q = jnp.einsum('bnh,oh->bno', feat_proj, q_w) + q_b
        k = jnp.einsum('bnh,oh->bno', feat_proj, k_w) + k_b
        logits = q + jnp.swapaxes(k, 2, 1)
        masked = logits + (1.0 - adj_mat) * NEG_INF
        masked = jnp.where(masked >= 0, masked, LEAKY_SLOPE * masked)
        atten = jax.nn.softmax(masked, axis=-1)
        out = jnp.einsum('bnm,bmh->bnh', atten, feat_proj)
        return out + feats

    def _L2_gnn_ref(hidden, adjacency, Wq, bq, Wk, bk, Wv, bv, Wo, bo, g1, b1, g2, b2, Wf1, bf1, Wf2, bf2):
        import jax, jax.numpy as jnp
        import numpy as np
        import math
        D_MODEL = 256
        NHEAD = 8
        HEAD_DIM = D_MODEL // NHEAD
        LN_EPS = 1e-05

        def _layernorm(x, g, b):
            mu = jnp.mean(x, axis=-1, keepdims=True)
            var = jnp.mean(jnp.square(x - mu), axis=-1, keepdims=True)
            return (x - mu) * jax.lax.rsqrt(var + LN_EPS) * g + b
        B, N, D = hidden.shape
        H, Hd = (NHEAD, HEAD_DIM)
        normed = _layernorm(hidden, g1, b1)
        q = (normed @ Wq + bq).reshape(B, N, H, Hd).transpose(0, 2, 1, 3)
        k = (normed @ Wk + bk).reshape(B, N, H, Hd).transpose(0, 2, 1, 3)
        v = (normed @ Wv + bv).reshape(B, N, H, Hd).transpose(0, 2, 1, 3)
        logits = jnp.einsum('bhnd,bhmd->bhnm', q, k) / math.sqrt(Hd)
        adj = adjacency[:, None, :, :]
        logits = logits + (2.0 * adj - 1.0)
        weights = jax.nn.softmax(logits, axis=-1)
        weights = weights * (0.25 + 0.75 * adj)
        weights = weights / jnp.maximum(weights.sum(axis=-1, keepdims=True), 1e-06)
        attended = jnp.einsum('bhnm,bhmd->bhnd', weights, v)
        attended = attended.transpose(0, 2, 1, 3).reshape(B, N, D)
        hidden = hidden + attended @ Wo + bo
        h2 = _layernorm(hidden, g2, b2)
        ff = jax.nn.gelu(h2 @ Wf1 + bf1, approximate=False) @ Wf2 + bf2
        return hidden + ff

    def _L3_gnn_ref(x, adj, Wq, bq, Wk, bk, Wv, bv, Wo, bo, gamma, beta):
        import jax, jax.numpy as jnp
        import numpy as np
        B, N, D, H = (8, 512, 256, 8)
        DK = D // H
        LN_EPS = 1e-05
        ADJ_MIN = 1e-08

        def _layer_norm(x, gamma, beta):
            mu = jnp.mean(x, axis=-1, keepdims=True)
            var = jnp.mean(jnp.square(x - mu), axis=-1, keepdims=True)
            return (x - mu) * jax.lax.rsqrt(var + LN_EPS) * gamma + beta
        b, n, d = x.shape
        q = (x @ Wq.T + bq).reshape(b, n, H, DK).transpose(0, 2, 1, 3)
        k = (x @ Wk.T + bk).reshape(b, n, H, DK).transpose(0, 2, 1, 3)
        v = (x @ Wv.T + bv).reshape(b, n, H, DK).transpose(0, 2, 1, 3)
        logits = jnp.einsum('bhqd,bhkd->bhqk', q, k) / np.sqrt(DK)
        logits = logits + jnp.log(jnp.clip(adj, ADJ_MIN, None))[:, None, :, :]
        attn = jax.nn.softmax(logits, axis=-1)
        out = jnp.einsum('bhqk,bhkd->bhqd', attn, v)
        out = out.transpose(0, 2, 1, 3).reshape(b, n, d)
        out = out @ Wo.T + bo
        return _layer_norm(x + out, gamma, beta)
    x = _L0_gnn_ref(x, adj, L0_gnn_W_q, L0_gnn_b_q, L0_gnn_W_k, L0_gnn_b_k, L0_gnn_W_v, L0_gnn_b_v, L0_gnn_w_g, L0_gnn_b_g)
    x = _L1_gnn_ref(x, adj, L1_gnn_fc_w, L1_gnn_fc_b, L1_gnn_q_w, L1_gnn_q_b, L1_gnn_k_w, L1_gnn_k_b)
    x = _L2_gnn_ref(x, adj, L2_gnn_Wq, L2_gnn_bq, L2_gnn_Wk, L2_gnn_bk, L2_gnn_Wv, L2_gnn_bv, L2_gnn_Wo, L2_gnn_bo, L2_gnn_g1, L2_gnn_b1, L2_gnn_g2, L2_gnn_b2, L2_gnn_Wf1, L2_gnn_bf1, L2_gnn_Wf2, L2_gnn_bf2)
    x = _L3_gnn_ref(x, adj, L3_gnn_Wq, L3_gnn_bq, L3_gnn_Wk, L3_gnn_bk, L3_gnn_Wv, L3_gnn_bv, L3_gnn_Wo, L3_gnn_bo, L3_gnn_gamma, L3_gnn_beta)
    return x

_drawn_inputs = setup_inputs


def setup_inputs(seed=0):
    import zlib

    import numpy as np

    out = dict(_drawn_inputs(seed))
    spreads = {'L0_gnn_b_q': (0.0, 0.1),
     'L0_gnn_b_k': (0.0, 0.8),
     'L0_gnn_b_v': (0.0, 0.1),
     'L2_gnn_bq': (0.0, 0.691),
     'L2_gnn_bk': (0.0, 0.8),
     'L2_gnn_bv': (0.0, 0.1),
     'L2_gnn_bo': (0.0, 0.1),
     'L2_gnn_g1': (1.0, 0.2),
     'L2_gnn_b1': (0.0, 0.1),
     'L2_gnn_g2': (1.0, 0.2),
     'L2_gnn_b2': (0.0, 0.1),
     'L2_gnn_bf1': (0.0, 0.1),
     'L2_gnn_bf2': (0.0, 0.1),
     'L3_gnn_bq': (0.0, 0.1),
     'L3_gnn_bk': (0.0, 0.8),
     'L3_gnn_bv': (0.0, 0.1),
     'L3_gnn_bo': (0.0, 0.1),
     'L3_gnn_gamma': (1.0, 0.2),
     'L3_gnn_beta': (0.0, 0.1)}
    factors = {}
    for name, (base, spread) in spreads.items():
        noise = np.random.default_rng([zlib.crc32(name.encode()), seed]).standard_normal(out[name].shape)
        drawn = base * np.exp(spread * noise) if base else spread * noise
        out[name] = jnp.asarray(drawn.astype(out[name].dtype))
    for name, factor in factors.items():
        out[name] = (out[name] * factor).astype(out[name].dtype)
    return out
```

```python
from contextlib import ExitStack

import concourse.bass as bass
from concourse import mybir

P = 128
B, N, D = 8, 1024, 256
H = 8
HD = D // H
F = 4 * D
NT = N // P
DC = D // P
FC = F // P
HG = 4
UNITS = H * NT
GROUPS = UNITS // 8
PAIRS = GROUPS // 2
HALF = 512
LAG = 3
PROBS = 4
SCALE = float(HD) ** -0.5
LN_EPS = 1e-5
LOG_EPS = 1e-9
ADJ_MIN = 1e-8
NEG_INF = -1e9
LEAK = 0.01
BIG = 3.0e38

ALU = mybir.AluOpType
ACT = mybir.ActivationFunctionType
F32 = mybir.dt.float32
F16 = mybir.dt.float16

STACK = [0, 2, 3]
LAST_STEP = 8 * (GROUPS - 1) + 22


class Ring:

    def __init__(self, banks):
        self.banks, self.index, self.owner, self.nth, self.count = banks, {}, [], [], {"act": 0, "dve": 0}

    def add(self, key, owner):
        self.index[key] = len(self.owner)
        self.owner.append(owner)
        self.count[owner] += 1
        self.nth.append(self.count[owner])

    def bank(self, key):
        return self.index[key] % self.banks

    def filled(self, key):
        return self.index[key] + 1

    def wait_free(self, eng, key, emptied):
        k = self.index[key] - self.banks
        if k >= 0:
            eng.wait_ge(emptied[self.owner[k]], self.nth[k])


def turn_ring():
    ring = Ring(3)

    def attention(a):
        for s in range(LAST_STEP + 1):
            u = s - LAG
            if 0 <= u < UNITS:
                ring.add((a, "P", u, 0), "act")
                ring.add((a, "P", u, 1), "act" if a == 1 else "dve")
            if s >= 20 and (s - 20) % 8 == 0:
                ring.add((a, "O", (s - 20) // 8), "dve")
            if a and s >= 29 and (s - 29) % 16 == 0:
                ring.add((a, "T", (s - 29) // 16), "act")
            if a and s >= 30 and (s - 30) % 16 == 0:
                ring.add((a, "W", (s - 30) // 16), "dve")

    attention(0)
    for t in range(NT):
        ring.add(("gat", t, 0), "act")
        ring.add(("gat", t, 1), "dve")
    attention(1)
    attention(2)
    return ring


def dense_ring():
    ring = Ring(4)
    for layer in range(4):
        for i in range(4):
            ring.add((layer, "xT", i), "act" if layer == 2 or i % 2 == 0 else "dve")
        if layer == 0:
            for i in range(2):
                ring.add((0, "c", i), "act")
        if layer == 1:
            for i in range(4):
                ring.add((1, "featT", i), "act")
            for i in range(2):
                ring.add((1, "k", i), "act")
            for i in range(4):
                ring.add((1, "feat", i), "dve")
        else:
            for i in range(8):
                ring.add((layer, "qk", i), "act")
            for i in range(4):
                ring.add((layer, "v", i), "dve")
        if layer == 2:
            for i in range(4):
                ring.add(("ffn", "xT", i), "act")
            for i in range(2 * FC):
                ring.add(("ffn", "up", i), "act")
            for i in range(4):
                ring.add(("ffn", "down", i), "dve")
    return ring


COLS = {}
_at = 0
for _name, _n in (("bq0", DC), ("bk0", DC), ("bq1", DC), ("bk1", DC), ("bq2", DC), ("bk2", DC), ("g1", DC),
                  ("b1", DC), ("g2", DC), ("b2", DC), ("bf1", FC), ("fcb", DC), ("kw", DC), ("wgc", DC),
                  ("bg", 1), ("qb", 1), ("kb", 1), ("sbq0", DC), ("sbq1", DC), ("sbq2", DC),
                  ("log_eps", 1), ("ln_eps", 1)):
    COLS[_name] = _at
    _at += _n
NCOLS = _at


def graph_layers(nc, t):
    ctx = ExitStack()

    def sb(name, shape, dt=F32):
        return ctx.enter_context(nc.sbuf_tensor(name, shape, dt))

    def sem(name):
        return ctx.enter_context(nc.semaphore(name))

    ident = sb("ident", [P, P])
    vec = sb("vec", [P, NCOLS])
    w_qkv = [sb(f"w_qkv{a}", [P, 3, DC, D]) for a in range(3)]
    w_o = [None] + [sb(f"w_o{a}", [P, DC, D]) for a in (1, 2)]
    w_fc = sb("w_fc", [P, DC, D])
    w_up = sb("w_up", [P, DC, F])
    w_down = sb("w_down", [P, FC, D])
    rows = sb("rows", [P, 11, D])
    R_BV, R_BO, R_BF2, R_GAMMA, R_BETA, R_WGA, R_FCB, R_QW = (0, 1, 2), (None, 3, 4), 5, 6, 7, 8, 9, 10
    wide = sb("wide", [P, 2, DC, P])

    x_sb = sb("x_sb", [P, NT, D])
    ring_adj = sb("ring_adj", [P, 4, N])
    pt = sb("pt", [P, 2, 8, NT, P])
    probs = sb("probs", [P, PROBS, N])
    q_cat = sb("q_cat", [P, H, N], F16)
    k_cat = sb("k_cat", [P, H, N], F16)
    v_sb = sb("v_sb", [P, NT, D])
    col_row = sb("col_row", [P, N])
    small = sb("small", [P, 256])
    o_turned = sb("o_turned", [P, 2 * P])
    o_nat = sb("o_nat", [P, 2, D])
    o_T = sb("o_T", [P, DC, 2 * P])

    flat = pt[:, :, :, :, :].rearrange("p a b c d -> p (a b c d)")
    xT = flat[:, 0:DC * N].rearrange("p (c n) -> p c n", c=DC)
    normed = flat[:, 2048:4096].rearrange("p (t d) -> p t d", t=NT)
    qk_f32 = flat[:, 4096:6144].rearrange("p (i n) -> p i n", i=4)
    parts = flat[:, 6144:10240].bitcast(F16).rearrange("p (w s g n) -> p w s g n", w=2, s=2, g=2)
    featT = flat[:, 10240:12288].rearrange("p (c n) -> p c n", c=DC)
    gat_pt = flat[:, 12288:14336].rearrange("p (b m n) -> p b m n", b=2, m=NT)
    act_up = flat[:, 8192:16384].rearrange("p (f n) -> p f n", f=FC)

    sums, gated = small[:, 0:64], small[:, 64:128]
    low, low2 = small[:, 128:136], small[:, 136:144]
    recip = small[:, 144:152]
    row_add = small[:, 152:160]
    stats = small[:, 160:208].rearrange("p (t s) -> p t s", t=NT)
    mean_var = small[:, 208:224].rearrange("p (t s) -> p t s", t=NT)
    std, rstd = small[:, 224:232], small[:, 232:240]
    low_units = sb("low_units", [P, PROBS])

    bank_sc = ctx.enter_context(nc.psum_tensor("bank_sc", [P, 4, HALF], F32))
    bank_tr = ctx.enter_context(nc.psum_tensor("bank_tr", [P, 3, HALF], F32))
    bank_o = ctx.enter_context(nc.psum_tensor("bank_o", [P, 2 * P], F32))

    def col(name, c=0):
        return vec[:, COLS[name] + c:COLS[name] + c + 1]

    raw = flat.rearrange("p (w c n) -> p w c n", c=DC, n=D)
    turned = [(t["L1_gnn_fc_w"], w_fc[:, :, :]), (t["L3_gnn_Wq"], w_qkv[2][:, 0]), (t["L3_gnn_Wk"], w_qkv[2][:, 1]),
              (t["L3_gnn_Wv"], w_qkv[2][:, 2]), (t["L3_gnn_Wo"], w_o[2][:, :, :])]
    w_in, id_zero, id_ready, w_turned, w_copied, consts = (sem("w_in"), sem("id_zero"), sem("id_ready"),
                                                           sem("w_turned"), sem("w_copied"), sem("consts"))
    chunks = lambda ap: ap.rearrange("(c p) n -> p c n", p=P)
    columns = [("bq0", "L0_gnn_b_q"), ("bk0", "L0_gnn_b_k"), ("bq1", "L2_gnn_bq"), ("bk1", "L2_gnn_bk"),
               ("bq2", "L3_gnn_bq"), ("bk2", "L3_gnn_bk"), ("g1", "L2_gnn_g1"), ("b1", "L2_gnn_b1"),
               ("g2", "L2_gnn_g2"), ("b2", "L2_gnn_b2"), ("bf1", "L2_gnn_bf1"), ("fcb", "L1_gnn_fc_b")]
    on_rows = [(R_BV[0], "L0_gnn_b_v"), (R_BV[1], "L2_gnn_bv"), (R_BV[2], "L3_gnn_bv"), (R_BO[1], "L2_gnn_bo"),
               (R_BO[2], "L3_gnn_bo"), (R_BF2, "L2_gnn_bf2"), (R_GAMMA, "L3_gnn_gamma"), (R_BETA, "L3_gnn_beta"),
               (R_FCB, "L1_gnn_fc_b")]
    loads = [(raw[:, i], chunks(w)) for i, (w, _) in enumerate(turned)]
    loads += [(w_qkv[0][:, i], chunks(t["L0_gnn_W_" + n])) for i, n in enumerate("qkv")]
    loads += [(w_qkv[1][:, i], chunks(t["L2_gnn_W" + n])) for i, n in enumerate("qkv")]
    loads += [(w_o[1][:, :, :], chunks(t["L2_gnn_Wo"])), (w_up[:, :, :], chunks(t["L2_gnn_Wf1"])),
              (w_down[:, :, :], chunks(t["L2_gnn_Wf2"]))]
    for name, source in columns:
        n = t[source].shape[0] // P
        loads.append((vec[:, COLS[name]:COLS[name] + n], t[source].rearrange("(c p) -> p c", p=P)))
    loads.append((vec[:, COLS["kw"]:COLS["kw"] + DC], t["L1_gnn_k_w"].rearrange("a (c p) -> p (a c)", p=P)))
    loads.append((vec[:, COLS["wgc"]:COLS["wgc"] + DC], t["L0_gnn_w_g"][D:2 * D].rearrange("(c p) -> p c", p=P)))
    loads += [(rows[:, r], t[source].partition_broadcast(P)) for r, source in on_rows]
    loads += [(rows[:, R_WGA], t["L0_gnn_w_g"][0:D].partition_broadcast(P)),
              (rows[:, R_QW], t["L1_gnn_q_w"].rearrange("a d -> (a d)").partition_broadcast(P)),
              (col("bg"), t["L0_gnn_b_g"].partition_broadcast(P)), (col("qb"), t["L1_gnn_q_b"].partition_broadcast(P)),
              (col("kb"), t["L1_gnn_k_b"].partition_broadcast(P))]

    with nc.allow_non_contiguous_dma(reason="small vectors, once"), nc.Block() as block:
        @block.sync
        def _(sp):
            for dst, src in loads:
                sp.dma_start(dst, src).then_inc(w_in, 16)
            sp.wait_ge(w_in, 16 * len(loads))

        @block.gpsimd
        def _(pool):
            pool.memset(ident[:, :], 0.0).then_inc(id_zero, 1)
            pool.wait_ge(id_zero, 1)
            pool.affine_select(out=ident[:, :], in_=ident[:, :], compare_op=ALU.not_equal, fill=1.0, base=0,
                               pattern=[[-1, P]], channel_multiplier=1).then_inc(id_ready, 1)

        @block.tensor
        def _(pe):
            pe.wait_ge(id_ready, 1)
            pe.wait_ge(w_in, 16 * len(loads))
            for i in range(len(turned)):
                if i >= 4:
                    pe.wait_ge(w_copied, i - 3)
                for ci in range(DC):
                    for co in range(DC):
                        last = pe.transpose(bank_sc[:, i % 4, (ci * DC + co) * P:(ci * DC + co + 1) * P],
                                            raw[:, i, co, ci * P:(ci + 1) * P], ident[:, :])
                last.then_inc(w_turned, 1)

        @block.vector
        def _(dve):
            dve.wait_ge(w_in, 16 * len(loads))
            for a in range(3):
                dve.tensor_scalar(vec[:, COLS[f"sbq{a}"]:COLS[f"sbq{a}"] + DC],
                                  vec[:, COLS[f"bq{a}"]:COLS[f"bq{a}"] + DC], SCALE, None, ALU.mult).then_inc(consts, 1)
            dve.memset(col("log_eps"), LOG_EPS).then_inc(consts, 1)
            dve.memset(col("ln_eps"), LN_EPS).then_inc(consts, 1)
            for w, name in enumerate(("wgc", "kw")):
                for c in range(DC):
                    dve.tensor_copy(wide[:, w, c], col(name, c).to_broadcast([P, P])).then_inc(consts, 1)
            for i, (_, dst) in enumerate(turned):
                dve.wait_ge(w_turned, i + 1)
                dve.tensor_copy(dst, bank_sc[:, i % 4, :].rearrange("p (c n) -> p c n", c=DC)).then_inc(w_copied, 1)
            dve.wait_ge(w_copied, len(turned))
            dve.wait_ge(consts, 9)

    turn, dense = turn_ring(), dense_ring()
    x_in = sem("x_in")
    adj_in = [sem(f"adj_in{i}") for i in range(4)]
    cat_in = [sem(f"cat_in{g}") for g in range(2)]
    y_out = sem("y_out")
    pe_dense, pe_scores, pe_turn, pe_pv = sem("pe_dense"), sem("pe_scores"), sem("pe_turn"), sem("pe_pv")
    dense_free = {"act": sem("dense_free_act"), "dve": sem("dense_free_dve")}
    turn_free = {"act": sem("turn_free_act"), "dve": sem("turn_free_dve")}
    v_low, v_gate, v_parts, v_x, v_rowadd, v_own = (sem("v_low"), sem("v_gate"), sem("v_parts"), sem("v_x"),
                                                    sem("v_rowadd"), sem("v_own"))
    v_stats, v_normed, v_leaky = sem("v_stats"), sem("v_normed"), sem("v_leaky")
    a_qk, a_exp, a_std, a_ln, a_o, a_line = (sem("a_qk"), sem("a_exp"), sem("a_std"), sem("a_ln"), sem("a_o"),
                                             sem("a_line"))
    p_clip, p_own, p_bias = sem("p_clip"), sem("p_own"), sem("p_bias")
    batch_sems = [x_in, *adj_in, *cat_in, y_out, pe_dense, pe_scores, pe_turn, pe_pv, *dense_free.values(),
                  *turn_free.values(), v_low, v_gate, v_parts, v_x, v_rowadd, v_own, v_stats, v_normed, v_leaky,
                  a_qk, a_exp, a_std, a_ln, a_o, a_line, p_clip, p_own, p_bias]

    X_DONE = [GROUPS, GROUPS + NT, GROUPS + NT + PAIRS, GROUPS + NT + 2 * PAIRS, GROUPS + NT + 3 * PAIRS]
    exps_before = [0, UNITS + NT, 2 * UNITS + NT]
    v_low_before = exps_before
    pvs_before = [0, GROUPS + NT, 2 * GROUPS + NT]

    def unit(u):
        p, g, n, j = u // 16, u // 8 % 2, u // 4 % 2, u % 4
        return p, g, n, HG * g + j, 2 * p + n

    def turned_by(a, group, owner):
        return max(turn.nth[turn.index[(a, "P", u, i)]] for u in range(8 * group, 8 * group + 8) for i in range(2)
                   if turn.owner[turn.index[(a, "P", u, i)]] == owner)

    with nc.Fori(0, B) as b:
        with nc.Block() as block:
            @block.sync
            def _(sp):
                sp.dma_start(x_sb[:, :, :], t["x"][bass.ds(b, 1)].rearrange("o (t p) d -> p (o t) d", p=P)
                             ).then_inc(x_in, 16)
                def load(i):
                    sp.dma_start(ring_adj[:, i % 4, :],
                                 t["adj"][bass.ds(b, 1), (i % NT) * P:(i % NT + 1) * P, :].rearrange(
                                     "o p m -> p (o m)")).then_inc(adj_in[i % 4], 16)

                def stack_parts(a):
                    for g in range(2):
                        for w, (cat, order) in enumerate(((q_cat, (0, 0, 1, 1)), (k_cat, (0, 1, 0, 1)))):
                            sp.wait_ge(v_parts, 8 * a + 4 * g + 2 * w + 2)
                            for j in range(HG):
                                for r, part in enumerate(order):
                                    sp.dma_start(cat[32 * r:32 * r + 32, HG * g + j, :],
                                                 parts[32 * j:32 * j + 32, w, part, g, :]).then_inc(cat_in[g], 16)

                for i in range(4):
                    load(i)
                stack_parts(0)
                for pair in range(1, 4 * PAIRS - 1):
                    last, q = (pair - 1) // PAIRS, (pair - 1) % PAIRS
                    if last == 1:
                        sp.wait_ge(v_low, UNITS + 2 * (q + 1))
                    elif last == 2:
                        sp.wait_ge(v_gate, 16 * (q + 1))
                    else:
                        sp.wait_ge(v_low, (0 if last == 0 else 2 * UNITS + NT) + 16 * (q + 1))
                    load(2 * pair + 2)
                    load(2 * pair + 3)
                    if pair == 2 * PAIRS:
                        stack_parts(1)
                    if pair == 3 * PAIRS:
                        stack_parts(2)
                sp.wait_ge(v_normed, 3 * NT)
                sp.dma_start(t["out"][bass.ds(b, 1)].rearrange("o (t p) d -> p (o t) d", p=P), normed
                             ).then_inc(y_out, 16)
                sp.wait_ge(y_out, 16)

            @block.gpsimd
            def _(pool):
                def clip(i):
                    tile = ring_adj[:, i % 4, :]
                    pool.wait_ge(adj_in[i % 4], 16 * (i // 4 + 1))
                    pool.tensor_scalar(tile, tile, ADJ_MIN, None, ALU.max).then_inc(p_clip, 1)

                def bias(i):
                    layer, n = i // NT, i % NT
                    tile = ring_adj[:, i % 4, :]
                    if layer == 0:
                        if n == 0:
                            pool.wait_ge(dense_free["act"], dense.nth[dense.index[(0, "c", 1)]])
                            pool.wait_ge(v_rowadd, 1)
                        pool.wait_ge(a_ln, n + 1)
                        pool.tensor_tensor(tile, tile, col_row[:, :], ALU.add).then_inc(p_own, 1)
                        pool.wait_ge(p_own, n + 1)
                        pool.tensor_scalar(tile, tile, row_add[:, n:n + 1], None, ALU.add).then_inc(p_bias, 1)
                    elif layer == 1:
                        pool.wait_ge(adj_in[i % 4], 16 * (i // 4 + 1))
                        pool.tensor_scalar(tile, tile, 1.0, -NEG_INF, ALU.subtract, ALU.mult).then_inc(p_bias, 1)
                    elif layer == 2:
                        pool.wait_ge(adj_in[i % 4], 16 * (i // 4 + 1))
                        pool.tensor_scalar(tile, tile, 2.0, -1.0, ALU.mult, ALU.add).then_inc(p_bias, 1)

                for i in range(4 * NT):
                    if i < 3 * NT:
                        bias(i)
                    else:
                        clip(i)

            @block.tensor
            def _(pe):
                def dense_out(key):
                    dense.wait_free(pe, key, dense_free)
                    return bank_sc[:, dense.bank(key), :]

                def turn_x(layer, src, wait):
                    wait()
                    for i in range(4):
                        out = dense_out((layer, "xT", i))
                        for q in range(4):
                            last = pe.transpose(out[:, q * P:(q + 1) * P],
                                                src[:, 4 * (i % 2) + q, (i // 2) * P:(i // 2 + 1) * P], ident[:, :])
                        last.then_inc(pe_dense, 1)

                def xT_there(layer):
                    for i in (2, 3):
                        k = dense.index[(layer, "xT", i)]
                        pe.wait_ge(dense_free[dense.owner[k]], dense.nth[k])

                def product(key, lhs, rhs, chunks=DC):
                    out = dense_out(key)
                    for c in range(chunks):
                        last = pe.matmul(out, lhs(c), rhs(c), start=(c == 0), stop=(c == chunks - 1))
                    last.then_inc(pe_dense, 1)

                def rows_product(key, lhs, rhs, chunks=DC):
                    out = dense_out(key)
                    for n in range(2):
                        for c in range(chunks):
                            last = pe.matmul(out[:, n * D:(n + 1) * D], lhs(n, c), rhs(c), start=(c == 0),
                                             stop=(c == chunks - 1))
                    last.then_inc(pe_dense, 1)

                def project(a):
                    layer = STACK[a]
                    w = w_qkv[a]
                    for i in range(8):
                        g, m, h = i // 4, i // 2 % 2, i % 2
                        product((layer, "qk", i), lambda c: w[:, m, c, g * P:(g + 1) * P],
                                lambda c: xT[:, c, h * HALF:(h + 1) * HALF])
                    for i in range(4):
                        rows_product((layer, "v", i), lambda n, c: xT[:, c, (2 * i + n) * P:(2 * i + n + 1) * P],
                                     lambda c: w[:, 2, c, :])

                def scores(a, u):
                    p, g, n, h, tile = unit(u)
                    if u % 8 == 0 and u < 16:
                        pe.wait_ge(cat_in[g], 16 * 32 * (a + 1))
                    if u == 0:
                        k = dense.index[(STACK[a], "qk", 7)]
                        pe.wait_ge(dense_free["act"], dense.nth[k])
                        pe.wait_ge(dense_free["dve"], dense.nth[dense.index[(STACK[a], "v", 3)]])
                    if u >= 2:
                        pe.wait_ge(v_low, v_low_before[a] + u - 1)
                    for h2 in range(2):
                        last = pe.matmul(bank_sc[:, 2 * (u % 2) + h2, :], q_cat[:, h, tile * P:(tile + 1) * P],
                                         k_cat[:, h, h2 * HALF:(h2 + 1) * HALF], start=True, stop=True)
                    last.then_inc(pe_scores, 1)

                def turn_probs(key, src, slot):
                    for i in range(2):
                        turn.wait_free(pe, (*key, i), turn_free)
                        for q in range(4):
                            last = pe.transpose(bank_tr[:, turn.bank((*key, i)), q * P:(q + 1) * P],
                                                src[:, (4 * i + q) * P:(4 * i + q + 1) * P], ident[:, :])
                        last.then_inc(pe_turn, 1)

                def attention(a):
                    for s in range(LAST_STEP + 1):
                        if s < UNITS:
                            scores(a, s)
                        u = s - LAG
                        if 0 <= u < UNITS:
                            if a == 1:
                                pe.wait_ge(v_gate, u + 1)
                            else:
                                pe.wait_ge(a_exp, exps_before[a] + u + 1)
                            turn_probs((a, "P", u), probs[:, u % PROBS, :], u)
                        group, m = (s - 11) // 8, (s - 11) % 8
                        tiles = [(0,), (1,), (2,), (3, 4), (5,), (6,), (7,), ()][m]
                        if 0 <= group < GROUPS:
                            if m == 0:
                                for owner in ("act", "dve"):
                                    if a != 1 or owner == "act":
                                        pe.wait_ge(turn_free[owner], turned_by(a, group, owner))
                                if a * GROUPS + group >= 1:
                                    pe.wait_ge(a_o, a * GROUPS + group)
                            g = group % 2
                            for m in tiles:
                                for j in range(HG):
                                    h = HG * g + j
                                    last = pe.matmul(
                                        bank_o[32 * j:32 * j + 32, :], v_sb[:, m, h * HD:(h + 1) * HD],
                                        pt[:, group % 2, :, m, :].rearrange("p (n j) q -> p n j q", n=2)[:, :, j, :],
                                        start=(m == 0), stop=(m == NT - 1), skip_group_check=True)
                            if NT - 1 in tiles:
                                last.then_inc(pe_pv, 1)
                        if s >= 20 and (s - 20) % 8 == 0:
                            group = (s - 20) // 8
                            key = (a, "O", group)
                            pe.wait_ge(a_o, a * GROUPS + group + 1)
                            turn.wait_free(pe, key, turn_free)
                            for n in range(2):
                                last = pe.transpose(bank_tr[:, turn.bank(key), n * P:(n + 1) * P],
                                                    o_turned[:, n * P:(n + 1) * P], ident[:, :])
                            last.then_inc(pe_turn, 1)
                        if a and s >= 29 and (s - 29) % 16 == 0:
                            pair = (s - 29) // 16
                            key = (a, "T", pair)
                            k = turn.index[(a, "O", 2 * pair + 1)]
                            pe.wait_ge(turn_free["dve"], turn.nth[k])
                            turn.wait_free(pe, key, turn_free)
                            for c in range(DC):
                                for n in range(2):
                                    last = pe.transpose(bank_tr[:, turn.bank(key), (2 * c + n) * P:(2 * c + n + 1) * P],
                                                        o_nat[:, n, c * P:(c + 1) * P], ident[:, :])
                            last.then_inc(pe_turn, 1)
                        if a and s >= 30 and (s - 30) % 16 == 0:
                            pair = (s - 30) // 16
                            key = (a, "W", pair)
                            pe.wait_ge(turn_free["act"], turn.nth[turn.index[(a, "T", pair)]])
                            turn.wait_free(pe, key, turn_free)
                            for n in range(2):
                                for c in range(DC):
                                    last = pe.matmul(bank_tr[:, turn.bank(key), n * D:(n + 1) * D],
                                                     o_T[:, c, n * P:(n + 1) * P], w_o[a][:, c, :],
                                                     start=(c == 0), stop=(c == DC - 1))
                            last.then_inc(pe_turn, 1)

                turn_x(0, x_sb, lambda: pe.wait_ge(x_in, 16))
                xT_there(0)
                for i in range(2):
                    product((0, "c", i), lambda c: wide[:, 0, c, :], lambda c: xT[:, c, i * HALF:(i + 1) * HALF])
                project(0)
                attention(0)

                turn_x(1, x_sb, lambda: pe.wait_ge(v_x, X_DONE[0]))
                xT_there(1)
                for i in range(4):
                    c, h = i // 2, i % 2
                    product((1, "featT", i), lambda k: w_fc[:, k, c * P:(c + 1) * P],
                            lambda k: xT[:, k, h * HALF:(h + 1) * HALF])
                for i in range(4):
                    pe.wait_ge(dense_free["act"], dense.nth[dense.index[(1, "featT", i)]])
                for i in range(2):
                    product((1, "k", i), lambda c: wide[:, 1, c, :], lambda c: featT[:, c, i * HALF:(i + 1) * HALF])
                for i in range(4):
                    rows_product((1, "feat", i), lambda n, c: xT[:, c, (2 * i + n) * P:(2 * i + n + 1) * P],
                                 lambda c: w_fc[:, c, :])
                for s in range(NT + 1):
                    if s < NT:
                        pe.wait_ge(a_exp, UNITS + s + 1)
                        turn_probs(("gat", s), probs[:, s % PROBS, :], s)
                    n = s - 1
                    if n >= 0:
                        for i in range(2):
                            k = turn.index[("gat", n, i)]
                            pe.wait_ge(turn_free[turn.owner[k]], turn.nth[k])
                        if n == 0:
                            pe.wait_ge(dense_free["dve"], dense.nth[dense.index[(1, "feat", 3)]])
                        if n >= 4:
                            pe.wait_ge(v_x, X_DONE[0] + n - 3)
                        for m in range(NT):
                            last = pe.matmul(bank_sc[:, n % 4, 0:D], gat_pt[:, n % 2, m, :], v_sb[:, m, :],
                                             start=(m == 0), stop=(m == NT - 1))
                        last.then_inc(pe_pv, 1)

                turn_x(2, normed, lambda: pe.wait_ge(v_normed, NT))
                xT_there(2)
                project(1)
                attention(1)
                turn_x("ffn", normed, lambda: pe.wait_ge(v_normed, 2 * NT))
                xT_there("ffn")
                for i in range(2 * FC):
                    f, h = i // 2, i % 2
                    product(("ffn", "up", i), lambda c: w_up[:, c, f * P:(f + 1) * P],
                            lambda c: xT[:, c, h * HALF:(h + 1) * HALF])
                pe.wait_ge(dense_free["act"], dense.nth[dense.index[("ffn", "up", 2 * FC - 1)]])
                for i in range(4):
                    rows_product(("ffn", "down", i), lambda n, f: act_up[:, f, (2 * i + n) * P:(2 * i + n + 1) * P],
                                 lambda f: w_down[:, f, :], FC)

                turn_x(3, x_sb, lambda: pe.wait_ge(v_x, X_DONE[3]))
                xT_there(3)
                project(2)
                attention(2)

            @block.scalar
            def _(act):
                def evacuate(key, dst, func=ACT.Copy, **kw):
                    act.wait_ge(pe_dense, dense.filled(key))
                    act.activation(dst, bank_sc[:, dense.bank(key), :], func, **kw).then_inc(dense_free["act"], 1)

                def take_xT(layer, gain=None, shift=None):
                    for i in range(4):
                        if dense.owner[dense.index[(layer, "xT", i)]] == "act":
                            c, h = i // 2, i % 2
                            dst = xT[:, c, h * HALF:(h + 1) * HALF]
                            if gain is None:
                                evacuate((layer, "xT", i), dst)
                            else:
                                evacuate((layer, "xT", i), dst, ACT.Identity, bias=col(shift, c), scale=col(gain, c))

                def take_qk(a):
                    for i in range(8):
                        g, m = i // 4, i // 2 % 2
                        if i >= 4:
                            act.wait_ge(v_parts, 8 * a + i - 3)
                        bias = col(f"bk{a}", g) if m else col(f"sbq{a}", g)
                        act.wait_ge(pe_dense, dense.filled((STACK[a], "qk", i)))
                        act.activation(qk_f32[:, i % 4, :], bank_sc[:, dense.bank((STACK[a], "qk", i)), :],
                                       ACT.Identity, bias=bias, scale=1.0 if m else SCALE
                                       ).then_inc(dense_free["act"], 1)

                def log(i):
                    tile = ring_adj[:, i % 4, :]
                    if i < NT:
                        act.wait_ge(adj_in[i % 4], 16 * (i // 4 + 1))
                        act.activation(tile, tile, ACT.Ln, bias=col("log_eps")).then_inc(a_ln, 1)
                    else:
                        act.wait_ge(p_clip, i - 3 * NT + 1)
                        act.activation(tile, tile, ACT.Ln).then_inc(a_ln, 1)

                def take_turned(key, dst):
                    act.wait_ge(pe_turn, turn.filled(key))
                    act.activation(dst, bank_tr[:, turn.bank(key), :], ACT.Copy).then_inc(turn_free["act"], 1)

                def attention(a):
                    first = STACK[a] * NT
                    for s in range(LAST_STEP + 1):
                        if s < UNITS:
                            act.wait_ge(v_low, v_low_before[a] + s + 1)
                            act.activation(probs[:, s % PROBS, :], probs[:, s % PROBS, :], ACT.Exp, scale=-1.0,
                                           bias=low_units[:, s % PROBS:s % PROBS + 1],
                                           accum_out=sums[:, s:s + 1]).then_inc(a_exp, 1)
                        u = s - LAG
                        if 0 <= u < UNITS:
                            group = u // 8
                            if u % 8 == 0 and group >= 2:
                                act.wait_ge(pe_pv, pvs_before[a] + group - 1)
                            for i in range(2 if a == 1 else 1):
                                take_turned((a, "P", u, i), pt[:, group % 2, u % 8, 4 * i:4 * i + 4, :])
                        if a != 1 and s % 16 in (8, 10) and s < 48:
                            log(first + 2 * (s // 16 + 1) + (s % 16 == 10))
                        if s >= 18 and (s - 18) % 8 == 0 and s < 8 * GROUPS + 18:
                            group = (s - 18) // 8
                            act.wait_ge(pe_pv, pvs_before[a] + group + 1)
                            if group >= 1:
                                act.wait_ge(pe_turn, turn.filled((a, "O", group - 1)))
                            act.activation(o_turned[:, :], bank_o[:, :], ACT.Copy).then_inc(a_o, 1)
                        if a and s >= 29 and (s - 29) % 16 == 0:
                            pair = (s - 29) // 16
                            if pair >= 1:
                                act.wait_ge(pe_turn, turn.filled((a, "W", pair - 1)))
                            take_turned((a, "T", pair), o_T[:, :, :].rearrange("p c n -> p (c n)"))

                def take_std(n):
                    act.wait_ge(v_stats, n + 1)
                    act.activation(std, mean_var[:, :, 1], ACT.Sqrt, bias=col("ln_eps")).then_inc(a_std, 1)

                take_xT(0)
                for i in range(2):
                    evacuate((0, "c", i), col_row[:, i * HALF:(i + 1) * HALF])
                take_qk(0)
                log(0)
                log(1)
                attention(0)

                take_xT(1)
                for i in range(4):
                    c, h = i // 2, i % 2
                    evacuate((1, "featT", i), featT[:, c, h * HALF:(h + 1) * HALF], ACT.Identity, bias=col("fcb", c))
                for i in range(2):
                    evacuate((1, "k", i), col_row[:, i * HALF:(i + 1) * HALF], ACT.Identity, bias=col("kb"))
                act.wait_ge(v_rowadd, 2)
                act.wait_ge(dense_free["act"], dense.nth[dense.index[(1, "k", 1)]])
                for s in range(NT + 2):
                    if s < NT:
                        if s >= PROBS:
                            act.wait_ge(pe_turn, turn.filled(("gat", s - PROBS, 1)))
                        act.activation(probs[:, s % PROBS, :], col_row[:, :], ACT.Identity,
                                       bias=row_add[:, s:s + 1]).then_inc(a_line, 1)
                    n = s - 1
                    if 0 <= n < NT:
                        act.wait_ge(v_leaky, n + 1)
                        act.activation(probs[:, n % PROBS, :], probs[:, n % PROBS, :], ACT.Exp, scale=-1.0,
                                       bias=low2[:, n:n + 1], accum_out=sums[:, n:n + 1]).then_inc(a_exp, 1)
                    n = s - 2
                    if n >= 0:
                        if n >= 2:
                            act.wait_ge(pe_pv, GROUPS + n - 1)
                        take_turned(("gat", n, 0), gat_pt[:, n % 2, 0:4, :])

                take_std(0)
                take_xT(2, "g1", "b1")
                take_qk(1)
                attention(1)
                take_std(1)
                take_xT("ffn", "g2", "b2")
                for i in range(2 * FC):
                    f, h = i // 2, i % 2
                    evacuate(("ffn", "up", i), act_up[:, f, h * HALF:(h + 1) * HALF], ACT.Gelu, bias=col("bf1", f))

                take_xT(3)
                take_qk(2)
                log(3 * NT)
                log(3 * NT + 1)
                attention(2)
                take_std(2)

            @block.vector
            def _(dve):
                own = [0]

                def link(ins):
                    own[0] += 1
                    ins.then_inc(v_own, 1)
                    dve.wait_ge(v_own, own[0])

                def take_xT(layer):
                    for i in range(4):
                        if dense.owner[dense.index[(layer, "xT", i)]] == "dve":
                            c, h = i // 2, i % 2
                            dve.wait_ge(pe_dense, dense.filled((layer, "xT", i)))
                            dve.tensor_copy(xT[:, c, h * HALF:(h + 1) * HALF],
                                            bank_sc[:, dense.bank((layer, "xT", i)), :]
                                            ).then_inc(dense_free["dve"], 1)

                def row_sums(src, r, add, product):
                    for n in range(NT):
                        last = dve.tensor_tensor_reduce(product[:, n % 2, :], src[:, n, :], rows[:, r, :], 1.0, 0.0,
                                                        ALU.mult, ALU.add, low[:, n:n + 1])
                        link(last)
                    dve.tensor_scalar(row_add, low, add, None, ALU.add).then_inc(v_rowadd, 1)

                def split_qk(a):
                    for i in range(8):
                        g, m, h = i // 4, i // 2 % 2, i % 2
                        k = dense.index[(STACK[a], "qk", i)]
                        dve.wait_ge(dense_free["act"], dense.nth[k])
                        hi, lo = (parts[:, m, s, g, h * HALF:(h + 1) * HALF] for s in range(2))
                        link(dve.tensor_copy(hi, qk_f32[:, i % 4, :]))
                        dve.tensor_tensor(lo, qk_f32[:, i % 4, :], hi, ALU.subtract).then_inc(v_parts, 1)

                def take_rows(key, i, r):
                    dve.wait_ge(pe_dense, dense.filled(key))
                    dve.tensor_tensor(v_sb[:, 2 * i:2 * i + 2, :],
                                      bank_sc[:, dense.bank(key), :].rearrange("p (n d) -> p n d", n=2),
                                      rows[:, r:r + 1, :].to_broadcast([P, 2, D]), ALU.add
                                      ).then_inc(dense_free["dve"], 1)

                def biased(a, u):
                    p, g, n, h, tile = unit(u)
                    dve.wait_ge(pe_scores, a * UNITS + u + 1)
                    if g == 0 and u % 16 in (0, 4):
                        i = STACK[a] * NT + tile
                        if a == 2:
                            dve.wait_ge(a_ln, NT + tile + 1)
                        else:
                            dve.wait_ge(p_bias, i + 1)
                    if u >= PROBS:
                        dve.wait_ge(pe_turn, turn.filled((a, "P", u - PROBS, 1)))
                    dve.tensor_tensor_reduce(probs[:, u % PROBS, :], bank_sc[:, 2 * (u % 2):2 * (u % 2) + 2, :],
                                             ring_adj[:, tile % 4, :], -1.0, BIG, ALU.add, ALU.min,
                                             low_units[:, u % PROBS:u % PROBS + 1]).then_inc(v_low, 1)

                def gate(u):
                    p, g, n, h, tile = unit(u)
                    dve.wait_ge(a_exp, exps_before[1] + u + 1)
                    dve.scalar_tensor_tensor(out=probs[:, u % PROBS, :], in0=ring_adj[:, tile % 4, :],
                                             scalar=5.0 / 3.0, in1=probs[:, u % PROBS, :], op0=ALU.add,
                                             op1=ALU.mult, accum_out=gated[:, u:u + 1]).then_inc(v_gate, 1)

                def finish(a, group):
                    g, p = group % 2, group // 2
                    of_group = slice(8 * group, 8 * group + 8)
                    if group >= 1:
                        dve.wait_ge(turn_free["dve"], turn.nth[turn.index[(a, "O", group - 1)]])
                    dve.wait_ge(a_exp, exps_before[a] + 8 * group + 8)
                    if a == 1:
                        dve.wait_ge(v_gate, 8 * group + 8)
                        link(dve.scalar_tensor_tensor(out=low, in0=sums[:, of_group], scalar=1e-6 * 8.0 / 3.0,
                                                      in1=gated[:, of_group], op0=ALU.mult, op1=ALU.max))
                        link(dve.reciprocal(recip, low))
                    else:
                        link(dve.reciprocal(recip, sums[:, of_group]))
                    key = (a, "O", group)
                    dve.wait_ge(pe_turn, turn.filled(key))
                    ins = dve.tensor_tensor(
                        o_nat[:, :, g * P:(g + 1) * P].rearrange("p n (j d) -> p n j d", j=HG),
                        bank_tr[:, turn.bank(key), 0:2 * P].rearrange("p (n j d) -> p n j d", n=2, j=HG),
                        recip.rearrange("p (n j) -> p n j", n=2).unsqueeze(3).to_broadcast([P, 2, HG, HD]), ALU.mult)
                    ins.then_inc(turn_free["dve"], 1)
                    if a == 0:
                        dve.wait_ge(turn_free["dve"], turn.nth[turn.index[key]])
                        xs = x_sb[:, 2 * p:2 * p + 2, g * P:(g + 1) * P]
                        dve.tensor_tensor(xs, xs, o_nat[:, :, g * P:(g + 1) * P], ALU.add).then_inc(v_x, 1)

                def project_out(a, pair):
                    key = (a, "W", pair)
                    xs = x_sb[:, 2 * pair:2 * pair + 2, :]
                    link(dve.tensor_tensor(xs, xs, rows[:, R_BO[a]:R_BO[a] + 1, :].to_broadcast([P, 2, D]), ALU.add))
                    dve.wait_ge(pe_turn, turn.filled(key))
                    dve.tensor_tensor(xs, xs, bank_tr[:, turn.bank(key), :].rearrange("p (n d) -> p n d", n=2),
                                      ALU.add).then_inc(turn_free["dve"], 1)
                    dve.wait_ge(turn_free["dve"], turn.nth[turn.index[key]])
                    dve.sem_inc(v_x, 1)

                def take_turned(key, dst):
                    dve.wait_ge(pe_turn, turn.filled(key))
                    dve.tensor_copy(dst, bank_tr[:, turn.bank(key), :].rearrange("p (m n) -> p m n", n=P)
                                    ).then_inc(turn_free["dve"], 1)

                def attention(a):
                    for s in range(LAST_STEP + 1):
                        if s < UNITS:
                            biased(a, s)
                        if a == 1 and 0 <= s - 1 < UNITS:
                            gate(s - 1)
                        u = s - LAG
                        if a != 1 and 0 <= u < UNITS:
                            group = u // 8
                            if u % 8 == 0 and group >= 2:
                                dve.wait_ge(pe_pv, pvs_before[a] + group - 1)
                            take_turned((a, "P", u, 1), pt[:, group % 2, u % 8, 4:8, :])
                        if s >= 20 and (s - 20) % 8 == 0:
                            finish(a, (s - 20) // 8)
                        if a and s >= 30 and (s - 30) % 16 == 0:
                            project_out(a, (s - 30) // 16)

                def norm(n):
                    for i in range(NT):
                        link(dve.bn_stats(stats[:, i, :], x_sb[:, i, :]))
                        ins = dve.bn_aggr(mean_var[:, i, :], stats[:, i, :])
                        link(ins)
                    dve.sem_inc(v_stats, 1)
                    dve.wait_ge(a_std, n + 1)
                    link(dve.reciprocal(rstd, std))
                    for i in range(NT):
                        ins = dve.tensor_scalar(normed[:, i, :], x_sb[:, i, :], mean_var[:, i, 0:1], rstd[:, i:i + 1],
                                                ALU.subtract, ALU.mult)
                        if n < 2:
                            ins.then_inc(v_normed, 1)
                        else:
                            link(ins)
                            link(dve.tensor_tensor(normed[:, i, :], normed[:, i, :], rows[:, R_GAMMA, :], ALU.mult))
                            dve.tensor_tensor(normed[:, i, :], normed[:, i, :], rows[:, R_BETA, :], ALU.add
                                              ).then_inc(v_normed, 1)
                    dve.wait_ge(v_normed, (n + 1) * NT)

                take_xT(0)
                dve.wait_ge(x_in, 16)
                row_sums(x_sb, R_WGA, col("bg"), o_nat)
                split_qk(0)
                for i in range(4):
                    take_rows((0, "v", i), i, R_BV[0])
                attention(0)

                dve.wait_ge(v_x, X_DONE[0])
                take_xT(1)
                for i in range(4):
                    take_rows((1, "feat", i), i, R_FCB)
                dve.wait_ge(dense_free["dve"], dense.nth[dense.index[(1, "feat", 3)]])
                row_sums(v_sb, R_QW, col("qb"), o_nat)
                for s in range(NT + 4):
                    if s < NT:
                        buf = probs[:, s % PROBS, :]
                        dve.wait_ge(a_line, s + 1)
                        dve.wait_ge(p_bias, NT + s + 1)
                        dve.tensor_tensor_reduce(buf, buf, ring_adj[:, s % 4, :], -1.0, BIG, ALU.add, ALU.min,
                                                 low[:, s:s + 1]).then_inc(v_low, 1)
                        dve.wait_ge(v_low, UNITS + s + 1)
                        link(dve.scalar_tensor_tensor(out=low2[:, s:s + 1], in0=low[:, s:s + 1], scalar=LEAK,
                                                      in1=low[:, s:s + 1], op0=ALU.mult, op1=ALU.min))
                        dve.scalar_tensor_tensor(out=buf, in0=buf, scalar=LEAK, in1=buf, op0=ALU.mult, op1=ALU.min
                                                 ).then_inc(v_leaky, 1)
                    n = s - 2
                    if 0 <= n < NT:
                        if n >= 2:
                            dve.wait_ge(pe_pv, GROUPS + n - 1)
                        take_turned(("gat", n, 1), gat_pt[:, n % 2, 4:8, :])
                    n = s - 4
                    if n >= 0:
                        dve.wait_ge(a_exp, UNITS + n + 1)
                        link(dve.reciprocal(recip[:, n:n + 1], sums[:, n:n + 1]))
                        dve.wait_ge(pe_pv, GROUPS + n + 1)
                        dve.scalar_tensor_tensor(out=x_sb[:, n, :], in0=bank_sc[:, n % 4, 0:D],
                                                 scalar=recip[:, n:n + 1], in1=x_sb[:, n, :], op0=ALU.mult,
                                                 op1=ALU.add).then_inc(v_x, 1)

                dve.wait_ge(v_x, X_DONE[1])
                norm(0)
                split_qk(1)
                for i in range(4):
                    take_rows((2, "v", i), i, R_BV[1])
                attention(1)
                norm(1)
                for i in range(4):
                    xs = x_sb[:, 2 * i:2 * i + 2, :]
                    link(dve.tensor_tensor(xs, xs, rows[:, R_BF2:R_BF2 + 1, :].to_broadcast([P, 2, D]), ALU.add))
                    dve.wait_ge(pe_dense, dense.filled(("ffn", "down", i)))
                    dve.tensor_tensor(xs, xs, bank_sc[:, dense.bank(("ffn", "down", i)), :].rearrange(
                        "p (n d) -> p n d", n=2), ALU.add).then_inc(dense_free["dve"], 1)
                    dve.wait_ge(dense_free["dve"], dense.nth[dense.index[("ffn", "down", i)]])
                    dve.sem_inc(v_x, 1)

                take_xT(3)
                split_qk(2)
                for i in range(4):
                    take_rows((3, "v", i), i, R_BV[2])
                attention(2)
                norm(2)

        for s in batch_sems:
            nc.sync.sem_clear(s)
        nc.all_engine_barrier()
    ctx.close()


INPUTS = ["x", "adj", "L0_gnn_W_q", "L0_gnn_b_q", "L0_gnn_W_k", "L0_gnn_b_k", "L0_gnn_W_v", "L0_gnn_b_v",
          "L0_gnn_w_g", "L0_gnn_b_g", "L1_gnn_fc_w", "L1_gnn_fc_b", "L1_gnn_q_w", "L1_gnn_q_b", "L1_gnn_k_w",
          "L1_gnn_k_b", "L2_gnn_Wq", "L2_gnn_bq", "L2_gnn_Wk", "L2_gnn_bk", "L2_gnn_Wv", "L2_gnn_bv", "L2_gnn_Wo",
          "L2_gnn_bo", "L2_gnn_g1", "L2_gnn_b1", "L2_gnn_g2", "L2_gnn_b2", "L2_gnn_Wf1", "L2_gnn_bf1", "L2_gnn_Wf2",
          "L2_gnn_bf2", "L3_gnn_Wq", "L3_gnn_bq", "L3_gnn_Wk", "L3_gnn_bk", "L3_gnn_Wv", "L3_gnn_bv", "L3_gnn_Wo",
          "L3_gnn_bo", "L3_gnn_gamma", "L3_gnn_beta"]


def kernel(**inputs):
    import numpy as _np
    import concourse.bacc as _bacc
    from concourse.bass_utils import run_bass_kernel_spmd as _run

    nc = _bacc.Bacc("TRN2", target_bir_lowering=False, num_devices=1)
    arrays, tensors = {}, {}
    for name in INPUTS:
        a = _np.ascontiguousarray(inputs[name])
        if a.ndim == 0:
            a = a.reshape(1)
        arrays[f"in_{name}"] = a
        tensors[name] = nc.dram_tensor(f"in_{name}", a.shape, mybir.dt.from_np(a.dtype), kind="ExternalInput").ap()
    tensors["out"] = nc.dram_tensor("out_0", (B, N, D), F32, kind="ExternalOutput").ap()
    graph_layers(nc, tensors)
    return _run(nc, [arrays], core_ids=[0]).results[0]["out_0"]
```

```python
from contextlib import ExitStack

import concourse.bass as bass
from concourse import mybir

P = 128
B, N, D = 8, 1024, 256
H = 8
HD = D // H
F = 4 * D
NT = N // P
DC = D // P
FC = F // P
HG = 4
UNITS = H * NT
GROUPS = UNITS // 8
PAIRS = GROUPS // 2
HALF = 512
LAG = 3
PROBS = 4
SCALE = float(HD) ** -0.5
LN_EPS = 1e-5
LOG_EPS = 1e-9
ADJ_MIN = 1e-8
NEG_INF = -1e9
LEAK = 0.01
BIG = 3.0e38
GATE_MIN = 1e-6

ALU = mybir.AluOpType
ACT = mybir.ActivationFunctionType
F32 = mybir.dt.float32
F16 = mybir.dt.float16

STACK = [0, 2, 3]
LAST_STEP = 8 * (GROUPS - 1) + 22


class Ring:

    def __init__(self, banks):
        self.banks, self.index, self.owner, self.nth, self.count = banks, {}, [], [], {"act": 0, "dve": 0}

    def add(self, key, owner):
        self.index[key] = len(self.owner)
        self.owner.append(owner)
        self.count[owner] += 1
        self.nth.append(self.count[owner])

    def bank(self, key):
        return self.index[key] % self.banks

    def filled(self, key):
        return self.index[key] + 1

    def wait_free(self, eng, key, emptied):
        k = self.index[key] - self.banks
        if k >= 0:
            eng.wait_ge(emptied[self.owner[k]], self.nth[k])


def turn_ring():
    ring = Ring(3)

    def attention(a):
        for s in range(LAST_STEP + 1):
            u = s - LAG
            if 0 <= u < UNITS:
                ring.add((a, "P", u, 0), "act")
                ring.add((a, "P", u, 1), "dve")
            if s >= 20 and (s - 20) % 8 == 0:
                ring.add((a, "O", (s - 20) // 8), "dve")
            if a and s >= 29 and (s - 29) % 16 == 0:
                ring.add((a, "T", (s - 29) // 16), "act")
            if a and s >= 30 and (s - 30) % 16 == 0:
                ring.add((a, "W", (s - 30) // 16), "dve")

    attention(0)
    for t in range(NT):
        ring.add(("gat", t, 0), "act")
        ring.add(("gat", t, 1), "dve")
    attention(1)
    attention(2)
    return ring


def projections(ring, layer):
    for i in range(4):
        ring.add((layer, "xT", i), "act" if layer == 2 or i % 2 == 0 else "dve")
    if layer == 0:
        for i in range(2):
            ring.add((0, "c", i), "act")
    for i in range(8):
        ring.add((layer, "qk", i), "act")
    for i in range(4):
        ring.add((layer, "v", i), "dve")


def first_ring():
    ring = Ring(4)
    projections(ring, 0)
    return ring


def dense_ring():
    ring = Ring(4)
    for i in range(4):
        ring.add((1, "xT", i), "act" if i % 2 == 0 else "dve")
    for i in range(4):
        ring.add((1, "feat", i), "dve")
    for i in range(4):
        ring.add((1, "featT", i), "act")
    for i in range(2):
        ring.add((1, "k", i), "act")
    projections(ring, 2)
    for i in range(4):
        ring.add(("ffn", "xT", i), "act")
    for i in range(2 * FC):
        ring.add(("ffn", "up", i), "act")
    for i in range(4):
        ring.add(("ffn", "down", i), "dve")
    projections(ring, 3)
    projections(ring, 0)
    return ring


COLS = {}
_at = 0
for _name, _n in (("bq0", DC), ("bk0", DC), ("bq1", DC), ("bk1", DC), ("bq2", DC), ("bk2", DC), ("g1", DC),
                  ("b1", DC), ("g2", DC), ("b2", DC), ("bf1", FC), ("fcb", DC), ("kw", DC), ("wgc", DC),
                  ("bg", 1), ("qb", 1), ("kb", 1), ("sbq0", DC), ("sbq1", DC), ("sbq2", DC),
                  ("log_eps", 1), ("minus_half", NT)):
    COLS[_name] = _at
    _at += _n
NCOLS = _at


def graph_layers(nc, t):
    ctx = ExitStack()

    def sb(name, shape, dt=F32):
        return ctx.enter_context(nc.sbuf_tensor(name, shape, dt))

    def sem(name):
        return ctx.enter_context(nc.semaphore(name))

    ident = sb("ident", [P, P])
    vec = sb("vec", [P, NCOLS])
    w_qkv = [sb(f"w_qkv{a}", [P, 3, DC, D]) for a in range(3)]
    w_o = [None] + [sb(f"w_o{a}", [P, DC, D]) for a in (1, 2)]
    w_fc = sb("w_fc", [P, DC, D])
    w_up = sb("w_up", [P, DC, F])
    w_down = sb("w_down", [P, FC, D])
    rows = sb("rows", [P, 11, D])
    R_BV, R_BO, R_BF2, R_GAMMA, R_BETA, R_WGA, R_FCB, R_QW = (0, 1, 2), (None, 3, 4), 5, 6, 7, 8, 9, 10
    wide = sb("wide", [P, 2, DC, P])

    x_sb = sb("x_sb", [P, NT, D])
    ring_adj = sb("ring_adj", [P, 4, N])
    pt = sb("pt", [P, 2, 8, NT, P])
    probs = sb("probs", [P, PROBS, N])
    q_cat = sb("q_cat", [P, H, N], F16)
    k_cat = sb("k_cat", [P, H, N], F16)
    v_sb = sb("v_sb", [P, NT, D])
    col_row = sb("col_row", [P, N])
    small = sb("small", [P, 256])
    o_turned = sb("o_turned", [P, 2 * P])
    o_nat = sb("o_nat", [P, 2, D])
    o_T = sb("o_T", [P, DC, 2 * P])

    spill = nc.dram_tensor("spill", (2, 2, 2, P, N), F16, kind="Internal").ap()

    flat = pt[:, :, :, :, :].rearrange("p a b c d -> p (a b c d)")
    xT = flat[:, 0:DC * N].rearrange("p (c n) -> p c n", c=DC)
    x_next = ring_adj[:, 0:2, :].rearrange("p s (t d) -> p (s t) d", d=D)
    normed = flat[:, 2048:4096].rearrange("p (t d) -> p t d", t=NT)
    qk_f32 = flat[:, 4096:6144].rearrange("p (i n) -> p i n", i=4)
    parts = flat[:, 6144:10240].bitcast(F16).rearrange("p (w s g n) -> p w s g n", w=2, s=2, g=2)
    products = flat[:, 2048:4096].rearrange("p (t d) -> p t d", t=NT)
    featT = flat[:, 10240:12288].rearrange("p (c n) -> p c n", c=DC)
    gat_pt = flat[:, 12288:14336].rearrange("p (b m n) -> p b m n", b=2, m=NT)
    y_sb = flat[:, 14336:16384].rearrange("p (t d) -> p t d", t=NT)
    act_up = flat[:, 8192:16384].rearrange("p (f n) -> p f n", f=FC)

    sums = small[:, 0:64]
    low, low2 = small[:, 128:136], small[:, 136:144]
    recip = small[:, 144:152]
    row_add = small[:, 152:160]
    stats = small[:, 160:208].rearrange("p (t s) -> p t s", t=NT)
    mean_var = small[:, 208:224].rearrange("p (t s) -> p t s", t=NT)
    var_eps, rstd = small[:, 224:232], small[:, 232:240]
    low_units = sb("low_units", [P, PROBS])

    bank_sc = ctx.enter_context(nc.psum_tensor("bank_sc", [P, 4, HALF], F32))
    bank_tr = ctx.enter_context(nc.psum_tensor("bank_tr", [P, 3, HALF], F32))
    bank_o = ctx.enter_context(nc.psum_tensor("bank_o", [P, 2 * P], F32))

    def col(name, c=0):
        return vec[:, COLS[name] + c:COLS[name] + c + 1]

    raw = flat.rearrange("p (w c n) -> p w c n", c=DC, n=D)
    turned = [(t["L1_gnn_fc_w"], w_fc[:, :, :]), (t["L3_gnn_Wq"], w_qkv[2][:, 0]), (t["L3_gnn_Wk"], w_qkv[2][:, 1]),
              (t["L3_gnn_Wv"], w_qkv[2][:, 2]), (t["L3_gnn_Wo"], w_o[2][:, :, :])]
    w_in, id_zero, id_ready, w_turned, w_copied, consts = (sem("w_in"), sem("id_zero"), sem("id_ready"),
                                                           sem("w_turned"), sem("w_copied"), sem("consts"))
    chunks = lambda ap: ap.rearrange("(c p) n -> p c n", p=P)
    columns = [("bq0", "L0_gnn_b_q"), ("bk0", "L0_gnn_b_k"), ("bq1", "L2_gnn_bq"), ("bk1", "L2_gnn_bk"),
               ("bq2", "L3_gnn_bq"), ("bk2", "L3_gnn_bk"), ("g1", "L2_gnn_g1"), ("b1", "L2_gnn_b1"),
               ("g2", "L2_gnn_g2"), ("b2", "L2_gnn_b2"), ("bf1", "L2_gnn_bf1"), ("fcb", "L1_gnn_fc_b")]
    on_rows = [(R_BV[0], "L0_gnn_b_v"), (R_BV[1], "L2_gnn_bv"), (R_BV[2], "L3_gnn_bv"), (R_BO[1], "L2_gnn_bo"),
               (R_BO[2], "L3_gnn_bo"), (R_BF2, "L2_gnn_bf2"), (R_GAMMA, "L3_gnn_gamma"), (R_BETA, "L3_gnn_beta"),
               (R_FCB, "L1_gnn_fc_b")]
    loads = [(raw[:, i], chunks(w)) for i, (w, _) in enumerate(turned)]
    loads += [(w_qkv[0][:, i], chunks(t["L0_gnn_W_" + n])) for i, n in enumerate("qkv")]
    loads += [(w_qkv[1][:, i], chunks(t["L2_gnn_W" + n])) for i, n in enumerate("qkv")]
    loads += [(w_o[1][:, :, :], chunks(t["L2_gnn_Wo"])), (w_up[:, :, :], chunks(t["L2_gnn_Wf1"])),
              (w_down[:, :, :], chunks(t["L2_gnn_Wf2"]))]
    for name, source in columns:
        n = t[source].shape[0] // P
        loads.append((vec[:, COLS[name]:COLS[name] + n], t[source].rearrange("(c p) -> p c", p=P)))
    loads.append((vec[:, COLS["kw"]:COLS["kw"] + DC], t["L1_gnn_k_w"].rearrange("a (c p) -> p (a c)", p=P)))
    loads.append((vec[:, COLS["wgc"]:COLS["wgc"] + DC], t["L0_gnn_w_g"][D:2 * D].rearrange("(c p) -> p c", p=P)))
    loads += [(rows[:, r], t[source].partition_broadcast(P)) for r, source in on_rows]
    loads += [(rows[:, R_WGA], t["L0_gnn_w_g"][0:D].partition_broadcast(P)),
              (rows[:, R_QW], t["L1_gnn_q_w"].rearrange("a d -> (a d)").partition_broadcast(P)),
              (col("bg"), t["L0_gnn_b_g"].partition_broadcast(P)), (col("qb"), t["L1_gnn_q_b"].partition_broadcast(P)),
              (col("kb"), t["L1_gnn_k_b"].partition_broadcast(P))]

    with nc.allow_non_contiguous_dma(reason="small vectors, once"), nc.Block() as block:
        @block.sync
        def _(sp):
            for dst, src in loads:
                sp.dma_start(dst, src).then_inc(w_in, 16)
            sp.wait_ge(w_in, 16 * len(loads))

        @block.gpsimd
        def _(pool):
            pool.memset(ident[:, :], 0.0).then_inc(id_zero, 1)
            pool.wait_ge(id_zero, 1)
            pool.affine_select(out=ident[:, :], in_=ident[:, :], compare_op=ALU.not_equal, fill=1.0, base=0,
                               pattern=[[-1, P]], channel_multiplier=1).then_inc(id_ready, 1)

        @block.tensor
        def _(pe):
            pe.wait_ge(id_ready, 1)
            pe.wait_ge(w_in, 16 * len(loads))
            for i in range(len(turned)):
                if i >= 4:
                    pe.wait_ge(w_copied, i - 3)
                for ci in range(DC):
                    for co in range(DC):
                        last = pe.transpose(bank_sc[:, i % 4, (ci * DC + co) * P:(ci * DC + co + 1) * P],
                                            raw[:, i, co, ci * P:(ci + 1) * P], ident[:, :])
                last.then_inc(w_turned, 1)

        @block.vector
        def _(dve):
            dve.wait_ge(w_in, 16 * len(loads))
            for a in range(3):
                dve.tensor_scalar(vec[:, COLS[f"sbq{a}"]:COLS[f"sbq{a}"] + DC],
                                  vec[:, COLS[f"bq{a}"]:COLS[f"bq{a}"] + DC], SCALE, None, ALU.mult).then_inc(consts, 1)
            dve.memset(col("log_eps"), LOG_EPS).then_inc(consts, 1)
            dve.memset(vec[:, COLS["minus_half"]:COLS["minus_half"] + NT], -0.5).then_inc(consts, 1)
            for w, name in enumerate(("wgc", "kw")):
                for c in range(DC):
                    dve.tensor_copy(wide[:, w, c], col(name, c).to_broadcast([P, P])).then_inc(consts, 1)
            for i, (_, dst) in enumerate(turned):
                dve.wait_ge(w_turned, i + 1)
                dve.tensor_copy(dst, bank_sc[:, i % 4, :].rearrange("p (c n) -> p c n", c=DC)).then_inc(w_copied, 1)
            dve.wait_ge(w_copied, len(turned))
            dve.wait_ge(consts, 9)

    turn, dense = turn_ring(), dense_ring()
    parts_out = [sem("q_parts_out"), sem("k_parts_out")]
    x_in, x_res_in = sem("x_in"), sem("x_res_in")
    adj_in = [sem(f"adj_in{i}") for i in range(4)]
    cat_in = [sem(f"cat_in{g}") for g in range(2)]
    y_out = sem("y_out")
    pe_dense, pe_scores, pe_turn, pe_pv = sem("pe_dense"), sem("pe_scores"), sem("pe_turn"), sem("pe_pv")
    dense_free = {"act": sem("dense_free_act"), "dve": sem("dense_free_dve")}
    turn_free = {"act": sem("turn_free_act"), "dve": sem("turn_free_dve")}
    v_low, v_parts, v_x, v_rowadd, v_own = (sem("v_low"), sem("v_parts"), sem("v_x"),
                                                    sem("v_rowadd"), sem("v_own"))
    v_stats, v_normed, v_leaky = sem("v_stats"), sem("v_normed"), sem("v_leaky")
    a_exp, a_ln, a_o, a_line = sem("a_exp"), sem("a_ln"), sem("a_o"), sem("a_line")
    p_gate = sem("p_gate")
    p_clip, p_own, p_bias, p_rstd = sem("p_clip"), sem("p_own"), sem("p_bias"), sem("p_rstd")
    batch_sems = [p_gate, *parts_out, x_in, *adj_in, *cat_in, pe_dense, pe_scores, pe_turn, pe_pv, *dense_free.values(),
                  *turn_free.values(), v_low, v_parts, v_x, v_rowadd, v_own, v_stats, v_normed, v_leaky,
                  a_exp, a_ln, a_o, a_line, p_clip, p_own, p_bias, p_rstd]

    late_cat, late_sems = sem("late_cat"), []
    late_sems += [late_cat, x_res_in, y_out]

    X_DONE = [GROUPS, GROUPS + NT, GROUPS + NT + PAIRS, GROUPS + NT + 2 * PAIRS, GROUPS + NT + 3 * PAIRS]
    exps_before = [0, UNITS + NT, 2 * UNITS + NT]
    v_low_before = exps_before
    pvs_before = [0, GROUPS + NT, 2 * GROUPS + NT]

    def unit(u):
        p, g, n, j = u // 16, u // 8 % 2, u // 4 % 2, u % 4
        return p, g, n, HG * g + j, 2 * p + n

    def turned_by(a, group, owner):
        return max(turn.nth[turn.index[(a, "P", u, i)]] for u in range(8 * group, 8 * group + 8) for i in range(2)
                   if turn.owner[turn.index[(a, "P", u, i)]] == owner)

    class Stage:

        def __init__(self, ring, parts, stacks, rowadd, adj, ln, own, bias):
            self.ring, self.parts, self.stacks, self.rowadd = ring, parts, stacks, rowadd
            self.adj, self.ln, self.own, self.bias = adj, ln, own, bias

    before_loop = Stage(first_ring(), parts=0, stacks=0, rowadd=0, adj=0, ln=0, own=0, bias=0)
    in_loop = Stage(dense, parts=16, stacks=2, rowadd=1, adj=4 * NT // 4 - 1, ln=3 * NT - 2, own=NT - 2,
                    bias=3 * NT - 2)

    def sp_load_adj(sp, item, i):
        sp.dma_start(ring_adj[:, i % 4, :], t["adj"][item, (i % NT) * P:(i % NT + 1) * P, :].rearrange(
            "o p m -> p (o m)")).then_inc(adj_in[i % 4], 16)

    def x_of(item):
        return t["x"][item].rearrange("o (t p) d -> p (o t) d", p=P)

    def sp_stack_parts(sp, parts_before, done):
        for g in range(2):
            for w in range(2):
                sp.wait_ge(v_parts, parts_before + 4 * g + 2 * w + 2)
                sp.dma_start(spill[w, g].rearrange("s p n -> p s n"), parts[:, w, :, g, :]).then_inc(parts_out[w], 16)
            for w, (cat, order) in enumerate(((q_cat, (0, 0, 1, 1)), (k_cat, (0, 1, 0, 1)))):
                sp.wait_ge(parts_out[w], 16 * (parts_before // 4 + g + 1))
                for r, part in enumerate(order):
                    sp.dma_start(cat[32 * r:32 * r + 32, HG * g:HG * g + HG, :],
                                 spill[w, g, part].rearrange("(j d) n -> d j n", j=HG)).then_inc(done[g], 16)

    STACK_DMAS = 8

    def sp_layer0(sp, item, st):
        sp_load_adj(sp, item, 2)
        sp_load_adj(sp, item, 3)
        sp.wait_ge(pe_dense, st.ring.filled((0, "xT", 3)))
        sp.wait_ge(v_rowadd, st.rowadd + 1)
        sp_load_adj(sp, item, 0)
        sp_load_adj(sp, item, 1)
        sp_stack_parts(sp, st.parts, (cat_in[0], late_cat))

    def sp_layer0_end(sp, st):
        for i in range(4):
            sp.wait_ge(adj_in[i], 16 * (st.adj + 1))
        sp.wait_ge(cat_in[0], 16 * STACK_DMAS * (st.stacks + 1))

    def pool_soul_bias(pool, n, ln, own):
        tile = ring_adj[:, n % 4, :]
        pool.wait_ge(a_ln, ln)
        pool.tensor_tensor(tile, tile, col_row[:, :], ALU.add).then_inc(p_own, 1)
        pool.wait_ge(p_own, own)
        pool.tensor_scalar(tile, tile, row_add[:, n:n + 1], None, ALU.add).then_inc(p_bias, 1)

    def pool_layer0(pool, st):
        pool.wait_ge(dense_free["act"], st.ring.nth[st.ring.index[(0, "c", 1)]])
        pool.wait_ge(v_rowadd, st.rowadd + 1)
        for n in range(2):
            pool_soul_bias(pool, n, st.ln + n + 1, st.own + n + 1)

    def pe_bank(pe, ring, key):
        ring.wait_free(pe, key, dense_free)
        return bank_sc[:, ring.bank(key), :]

    def pe_turn_x(pe, ring, layer, src, ready=None):
        for i in range(4):
            if ready is not None:
                ready(i // 2)
            out = pe_bank(pe, ring, (layer, "xT", i))
            for q in range(4):
                last = pe.transpose(out[:, q * P:(q + 1) * P],
                                    src[:, 4 * (i // 2) + q, (i % 2) * P:(i % 2 + 1) * P], ident[:, :])
            last.then_inc(pe_dense, 1)

    def pe_xT_there(pe, ring, layer, halves=(0, 1)):
        for h in halves:
            for i in (2 * h, 2 * h + 1):
                k = ring.index[(layer, "xT", i)]
                pe.wait_ge(dense_free[ring.owner[k]], ring.nth[k])

    def pe_product(pe, ring, key, lhs, rhs, chunks=DC):
        out = pe_bank(pe, ring, key)
        for c in range(chunks):
            last = pe.matmul(out, lhs(c), rhs(c), start=(c == 0), stop=(c == chunks - 1))
        last.then_inc(pe_dense, 1)

    def pe_rows_product(pe, ring, key, lhs, rhs, chunks=DC):
        out = pe_bank(pe, ring, key)
        for n in range(2):
            for c in range(chunks):
                last = pe.matmul(out[:, n * D:(n + 1) * D], lhs(n, c), rhs(c), start=(c == 0), stop=(c == chunks - 1))
        last.then_inc(pe_dense, 1)

    def pe_project(pe, ring, a):
        layer, w = STACK[a], w_qkv[a]
        for i in range(8):
            g, m, h = i // 4, i // 2 % 2, i % 2
            pe_product(pe, ring, (layer, "qk", i), lambda c: w[:, m, c, g * P:(g + 1) * P],
                       lambda c: xT[:, c, h * HALF:(h + 1) * HALF])
        for i in range(4):
            pe_rows_product(pe, ring, (layer, "v", i), lambda n, c: xT[:, c, (2 * i + n) * P:(2 * i + n + 1) * P],
                            lambda c: w[:, 2, c, :])

    def pe_layer0_start(pe, st):
        pe.wait_ge(x_in, 16)
        pe_turn_x(pe, st.ring, 0, x_next)
        pe_xT_there(pe, st.ring, 0)
        for i in range(2):
            pe_product(pe, st.ring, (0, "c", i), lambda c: wide[:, 0, c, :],
                       lambda c: xT[:, c, i * HALF:(i + 1) * HALF])

    def act_evacuate(act, ring, key, dst, func=ACT.Copy, **kw):
        act.wait_ge(pe_dense, ring.filled(key))
        act.activation(dst, bank_sc[:, ring.bank(key), :], func, **kw).then_inc(dense_free["act"], 1)

    def act_take_xT(act, ring, layer, gain=None, shift=None):
        for i in range(4):
            if ring.owner[ring.index[(layer, "xT", i)]] == "act":
                h, c = i // 2, i % 2
                dst = xT[:, c, h * HALF:(h + 1) * HALF]
                if gain is None:
                    act_evacuate(act, ring, (layer, "xT", i), dst)
                else:
                    act_evacuate(act, ring, (layer, "xT", i), dst, ACT.Identity, bias=col(shift, c), scale=col(gain, c))

    def act_take_qk(act, ring, a, parts_before):
        for i in range(8):
            g, m = i // 4, i // 2 % 2
            if i >= 4:
                act.wait_ge(v_parts, parts_before + i - 3)
            bias = col(f"bk{a}", g) if m else col(f"sbq{a}", g)
            act_evacuate(act, ring, (STACK[a], "qk", i), qk_f32[:, i % 4, :], ACT.Identity, bias=bias,
                         scale=1.0 if m else SCALE)

    def act_layer0_start(act, st):
        act_take_xT(act, st.ring, 0)
        for i in range(2):
            act_evacuate(act, st.ring, (0, "c", i), col_row[:, i * HALF:(i + 1) * HALF])

    def act_layer0_end(act, st):
        act_take_qk(act, st.ring, 0, st.parts)
        for n in range(2):
            act.wait_ge(adj_in[n], 16 * (st.adj + 1))
            act.activation(ring_adj[:, n, :], ring_adj[:, n, :], ACT.Ln, bias=col("log_eps")).then_inc(a_ln, 1)

    class Own:

        def __init__(self, dve):
            self.dve, self.n = dve, 0

        def mark(self, ins):
            self.n += 1
            ins.then_inc(v_own, 1)

        def wait(self):
            self.dve.wait_ge(v_own, self.n)

        def link(self, ins):
            self.mark(ins)
            self.wait()

    def dve_take_xT(dve, ring, layer):
        for i in range(4):
            if ring.owner[ring.index[(layer, "xT", i)]] == "dve":
                h, c = i // 2, i % 2
                dve.wait_ge(pe_dense, ring.filled((layer, "xT", i)))
                dve.tensor_copy(xT[:, c, h * HALF:(h + 1) * HALF], bank_sc[:, ring.bank((layer, "xT", i)), :]
                                ).then_inc(dense_free["dve"], 1)

    def dve_row_sums(dve, own, src, r, add):
        for n in range(NT):
            own.mark(dve.tensor_tensor_reduce(products[:, n, :], src[:, n, :], rows[:, r, :], 1.0, 0.0, ALU.mult,
                                              ALU.add, low[:, n:n + 1]))
        own.wait()
        dve.tensor_scalar(row_add, low, add, None, ALU.add).then_inc(v_rowadd, 1)

    def dve_split_qk(dve, own, ring, a):
        for i in range(8):
            g, m, h = i // 4, i // 2 % 2, i % 2
            dve.wait_ge(dense_free["act"], ring.nth[ring.index[(STACK[a], "qk", i)]])
            hi, lo = (parts[:, m, s, g, h * HALF:(h + 1) * HALF] for s in range(2))
            own.link(dve.tensor_copy(hi, qk_f32[:, i % 4, :]))
            dve.tensor_tensor(lo, qk_f32[:, i % 4, :], hi, ALU.subtract).then_inc(v_parts, 1)

    def dve_take_rows(dve, ring, key, i, r):
        dve.wait_ge(pe_dense, ring.filled(key))
        dve.tensor_tensor(v_sb[:, 2 * i:2 * i + 2, :],
                          bank_sc[:, ring.bank(key), :].rearrange("p (n d) -> p n d", n=2),
                          rows[:, r:r + 1, :].to_broadcast([P, 2, D]), ALU.add).then_inc(dense_free["dve"], 1)

    def dve_layer0_start(dve, own, st):
        dve_take_xT(dve, st.ring, 0)
        dve.wait_ge(x_in, 16)
        dve_row_sums(dve, own, x_next, R_WGA, col("bg"))

    def dve_layer0_end(dve, own, st):
        dve_split_qk(dve, own, st.ring, 0)
        for i in range(4):
            dve_take_rows(dve, st.ring, (0, "v", i), i, R_BV[0])

    with nc.Block() as block:
        @block.sync
        def _(sp):
            sp.dma_start(x_next, x_of(slice(0, 1))).then_inc(x_in, 16)
            sp.dma_start(x_sb[:, :, :], x_of(slice(0, 1))).then_inc(x_res_in, 16)
            sp_layer0(sp, slice(0, 1), before_loop)
            sp_layer0_end(sp, before_loop)
            sp.sem_inc(y_out, 16)

        @block.gpsimd
        def _(pool):
            pool_layer0(pool, before_loop)

        @block.tensor
        def _(pe):
            pe_layer0_start(pe, before_loop)
            pe_project(pe, before_loop.ring, 0)

        @block.scalar
        def _(act):
            act.preload_act_table_set("natural_log_exp_and_others")
            act_layer0_start(act, before_loop)
            act_layer0_end(act, before_loop)

        @block.vector
        def _(dve):
            own = Own(dve)
            dve_layer0_start(dve, own, before_loop)
            dve_layer0_end(dve, own, before_loop)

    def clear_semaphores():
        for s in batch_sems:
            nc.sync.sem_clear(s)
        nc.all_engine_barrier()

    clear_semaphores()

    with nc.Fori(0, B) as b:
        next_item = bass.ds((b + 1) % B, 1)
        with nc.Block() as block:
            @block.sync
            def _(sp):
                for pair in range(1, 4 * PAIRS - 1):
                    last, q = (pair - 1) // PAIRS, (pair - 1) % PAIRS
                    if last == 1:
                        sp.wait_ge(v_low, UNITS + 2 * (q + 1))
                    else:
                        sp.wait_ge(v_low, (0, None, UNITS + NT, 2 * UNITS + NT)[last] + 16 * (q + 1))
                    sp_load_adj(sp, bass.ds(b, 1), 2 * pair + 2)
                    sp_load_adj(sp, bass.ds(b, 1), 2 * pair + 3)
                    if pair in (1, 2, 3):
                        sp.sem_clear((late_cat, y_out, x_res_in)[pair - 1])
                    if pair == 2 * PAIRS:
                        sp_stack_parts(sp, 0, cat_in)
                    if pair == 3 * PAIRS:
                        sp_stack_parts(sp, 8, cat_in)
                sp.wait_ge(v_low, 2 * UNITS + NT + 48)
                sp.dma_start(x_next, x_of(next_item)).then_inc(x_in, 16)
                sp.wait_ge(v_low, 3 * UNITS + NT)
                sp_layer0(sp, next_item, in_loop)
                sp.wait_ge(v_normed, 3 * NT)
                sp.dma_start(x_sb[:, :, :], x_of(next_item)).then_inc(x_res_in, 16)
                sp.dma_start(t["out"][bass.ds(b, 1)].rearrange("o (t p) d -> p (o t) d", p=P), y_sb
                             ).then_inc(y_out, 16)
                sp_layer0_end(sp, in_loop)

            @block.gpsimd
            def _(pool):
                def clip(i):
                    tile = ring_adj[:, i % 4, :]
                    pool.wait_ge(adj_in[i % 4], 16 * (i // 4))
                    pool.tensor_scalar(tile, tile, ADJ_MIN, None, ALU.max).then_inc(p_clip, 1)

                def bias(i):
                    tile = ring_adj[:, i % 4, :]
                    if i < NT:
                        pool_soul_bias(pool, i, i - 1, i - 1)
                        return
                    pool.wait_ge(adj_in[i % 4], 16 * (i // 4))
                    if i < 2 * NT:
                        pool.tensor_scalar(tile, tile, 1.0, -NEG_INF, ALU.subtract, ALU.mult).then_inc(p_bias, 1)
                        return
                    k, gate = i - 2 * NT, col_row[:, :]
                    if k == 0:
                        pool.wait_ge(a_line, NT)
                    else:
                        pool.wait_ge(p_bias, i - 2)
                    pool.tensor_scalar(gate, tile, 0.75, 0.25, ALU.mult, ALU.add).then_inc(p_gate, 1)
                    pool.wait_ge(p_gate, 3 * k + 1)
                    pool.tensor_scalar(gate, gate, GATE_MIN, None, ALU.max).then_inc(p_gate, 1)
                    pool.tensor_scalar(tile, tile, 2.0, -1.0, ALU.mult, ALU.add).then_inc(p_gate, 1)
                    pool.wait_ge(p_gate, 3 * k + 3)
                    pool.wait_ge(a_ln, NT - 2 + k + 1)
                    pool.tensor_tensor(tile, tile, gate, ALU.add).then_inc(p_bias, 1)

                def reciprocal_std(n):
                    pool.wait_ge(v_stats, n + 1)
                    pool.tensor_tensor(rstd, var_eps, vec[:, COLS["minus_half"]:COLS["minus_half"] + NT], ALU.pow
                                       ).then_inc(p_rstd, 1)

                for i in range(2, 2 * NT):
                    bias(i)
                reciprocal_std(0)
                for i in range(2 * NT, 3 * NT):
                    bias(i)
                clip(3 * NT)
                clip(3 * NT + 1)
                reciprocal_std(1)
                for i in range(3 * NT + 2, 4 * NT):
                    clip(i)
                reciprocal_std(2)
                pool_layer0(pool, in_loop)

            @block.tensor
            def _(pe):
                def scores(a, u):
                    p, g, n, h, tile = unit(u)
                    if a == 0 and u == 8:
                        pe.wait_ge(late_cat, 16 * STACK_DMAS)
                    if a and u % 8 == 0 and u < 16:
                        pe.wait_ge(cat_in[g], 16 * STACK_DMAS * a)
                    if a and u == 0:
                        k = dense.index[(STACK[a], "qk", 7)]
                        pe.wait_ge(dense_free["act"], dense.nth[k])
                        pe.wait_ge(dense_free["dve"], dense.nth[dense.index[(STACK[a], "v", 3)]])
                    if u >= 2:
                        pe.wait_ge(v_low, v_low_before[a] + u - 1)
                    for h2 in range(2):
                        last = pe.matmul(bank_sc[:, 2 * (u % 2) + h2, :], q_cat[:, h, tile * P:(tile + 1) * P],
                                         k_cat[:, h, h2 * HALF:(h2 + 1) * HALF], start=True, stop=True)
                    last.then_inc(pe_scores, 1)

                def turn_probs(key, src, slot):
                    for i in range(2):
                        turn.wait_free(pe, (*key, i), turn_free)
                        for q in range(4):
                            last = pe.transpose(bank_tr[:, turn.bank((*key, i)), q * P:(q + 1) * P],
                                                src[:, (4 * i + q) * P:(4 * i + q + 1) * P], ident[:, :])
                        last.then_inc(pe_turn, 1)

                def attention(a, meanwhile=None):
                    for s in range(LAST_STEP + 1):
                        if s < UNITS:
                            scores(a, s)
                        u = s - LAG
                        if 0 <= u < UNITS:
                            pe.wait_ge(a_exp, exps_before[a] + u + 1)
                            turn_probs((a, "P", u), probs[:, u % PROBS, :], u)
                        group, m = (s - 11) // 8, (s - 11) % 8
                        tiles = [(0,), (1,), (2,), (3, 4), (5,), (6,), (7,), ()][m]
                        if 0 <= group < GROUPS:
                            if m == 0:
                                for owner in ("act", "dve"):
                                    pe.wait_ge(turn_free[owner], turned_by(a, group, owner))
                                if a * GROUPS + group >= 1:
                                    pe.wait_ge(a_o, a * GROUPS + group)
                            g = group % 2
                            for m in tiles:
                                for j in range(HG):
                                    h = HG * g + j
                                    last = pe.matmul(
                                        bank_o[32 * j:32 * j + 32, :], v_sb[:, m, h * HD:(h + 1) * HD],
                                        pt[:, group % 2, :, m, :].rearrange("p (n j) q -> p n j q", n=2)[:, :, j, :],
                                        start=(m == 0), stop=(m == NT - 1), skip_group_check=True)
                            if NT - 1 in tiles:
                                last.then_inc(pe_pv, 1)
                        if s == LAST_STEP - 4 and meanwhile:
                            meanwhile()
                        if s >= 20 and (s - 20) % 8 == 0:
                            group = (s - 20) // 8
                            key = (a, "O", group)
                            pe.wait_ge(a_o, a * GROUPS + group + 1)
                            turn.wait_free(pe, key, turn_free)
                            for n in range(2):
                                last = pe.transpose(bank_tr[:, turn.bank(key), n * P:(n + 1) * P],
                                                    o_turned[:, n * P:(n + 1) * P], ident[:, :])
                            last.then_inc(pe_turn, 1)
                        if a and s >= 29 and (s - 29) % 16 == 0:
                            pair = (s - 29) // 16
                            key = (a, "T", pair)
                            k = turn.index[(a, "O", 2 * pair + 1)]
                            pe.wait_ge(turn_free["dve"], turn.nth[k])
                            turn.wait_free(pe, key, turn_free)
                            for c in range(DC):
                                for n in range(2):
                                    last = pe.transpose(bank_tr[:, turn.bank(key), (2 * c + n) * P:(2 * c + n + 1) * P],
                                                        o_nat[:, n, c * P:(c + 1) * P], ident[:, :])
                            last.then_inc(pe_turn, 1)
                        if a and s >= 30 and (s - 30) % 16 == 0:
                            pair = (s - 30) // 16
                            key = (a, "W", pair)
                            pe.wait_ge(turn_free["act"], turn.nth[turn.index[(a, "T", pair)]])
                            turn.wait_free(pe, key, turn_free)
                            for n in range(2):
                                for c in range(DC):
                                    last = pe.matmul(bank_tr[:, turn.bank(key), n * D:(n + 1) * D],
                                                     o_T[:, c, n * P:(n + 1) * P], w_o[a][:, c, :],
                                                     start=(c == 0), stop=(c == DC - 1))
                            last.then_inc(pe_turn, 1)

                attention(0)

                pe.wait_ge(v_x, X_DONE[0])
                pe_turn_x(pe, dense, 1, x_sb)
                pe_xT_there(pe, dense, 1)
                for i in range(4):
                    pe_rows_product(pe, dense, (1, "feat", i), lambda n, c: xT[:, c, (2 * i + n) * P:(2 * i + n + 1) * P],
                                    lambda c: w_fc[:, c, :])
                for i in range(4):
                    c, h = i // 2, i % 2
                    pe_product(pe, dense, (1, "featT", i), lambda k: w_fc[:, k, c * P:(c + 1) * P],
                               lambda k: xT[:, k, h * HALF:(h + 1) * HALF])
                pe.wait_ge(dense_free["act"], dense.nth[dense.index[(1, "featT", 3)]])
                for i in range(2):
                    pe_product(pe, dense, (1, "k", i), lambda c: wide[:, 1, c, :],
                               lambda c: featT[:, c, i * HALF:(i + 1) * HALF])
                for s in range(NT + 1):
                    if s < NT:
                        pe.wait_ge(a_exp, UNITS + s + 1)
                        turn_probs(("gat", s), probs[:, s % PROBS, :], s)
                    n = s - 1
                    if n >= 0:
                        for i in range(2):
                            k = turn.index[("gat", n, i)]
                            pe.wait_ge(turn_free[turn.owner[k]], turn.nth[k])
                        if n == 0:
                            pe.wait_ge(dense_free["dve"], dense.nth[dense.index[(1, "feat", 3)]])
                            pe.wait_ge(dense_free["act"], dense.nth[dense.index[(1, "k", 1)]])
                        if n >= 4:
                            pe.wait_ge(v_x, X_DONE[0] + n - 3)
                        for m in range(NT):
                            last = pe.matmul(bank_sc[:, n % 4, 0:D], gat_pt[:, n % 2, m, :], v_sb[:, m, :],
                                             start=(m == 0), stop=(m == NT - 1))
                        last.then_inc(pe_pv, 1)

                pe_turn_x(pe, dense, 2, normed, lambda h: pe.wait_ge(v_normed, 4 * (h + 1)))
                pe_xT_there(pe, dense, 2)
                pe_project(pe, dense, 1)
                attention(1)
                pe_turn_x(pe, dense, "ffn", normed, lambda h: pe.wait_ge(v_normed, NT + 4 * (h + 1)))
                pe_xT_there(pe, dense, "ffn")
                for i in range(2 * FC):
                    f, h = i // 2, i % 2
                    pe_product(pe, dense, ("ffn", "up", i), lambda c: w_up[:, c, f * P:(f + 1) * P],
                               lambda c: xT[:, c, h * HALF:(h + 1) * HALF])
                pe.wait_ge(dense_free["act"], dense.nth[dense.index[("ffn", "up", 2 * FC - 1)]])
                for i in range(4):
                    pe_rows_product(pe, dense, ("ffn", "down", i),
                                    lambda n, f: act_up[:, f, (2 * i + n) * P:(2 * i + n + 1) * P],
                                    lambda f: w_down[:, f, :], FC)

                pe_turn_x(pe, dense, 3, x_sb, lambda h: pe.wait_ge(v_x, X_DONE[2] + 2 * (h + 1)))
                pe_xT_there(pe, dense, 3)
                pe_project(pe, dense, 2)
                attention(2, lambda: pe_layer0_start(pe, in_loop))
                pe_project(pe, dense, 0)

            @block.scalar
            def _(act):
                def log(i):
                    tile = ring_adj[:, i % 4, :]
                    if i < NT:
                        if i >= 4:
                            act.wait_ge(adj_in[i % 4], 16 * (i // 4))
                        act.activation(tile, tile, ACT.Ln, bias=col("log_eps")).then_inc(a_ln, 1)
                    elif i < 3 * NT:
                        act.wait_ge(p_gate, 3 * (i - 2 * NT) + 2)
                        act.activation(col_row[:, :], col_row[:, :], ACT.Ln).then_inc(a_ln, 1)
                    else:
                        act.wait_ge(p_clip, i - 3 * NT + 1)
                        act.activation(tile, tile, ACT.Ln).then_inc(a_ln, 1)

                def take_turned(key, dst):
                    act.wait_ge(pe_turn, turn.filled(key))
                    act.activation(dst, bank_tr[:, turn.bank(key), :], ACT.Copy).then_inc(turn_free["act"], 1)

                def attention(a, meanwhile=None):
                    first = STACK[a] * NT
                    for s in range(LAST_STEP + 1):
                        u = s - LAG
                        if 0 <= u < UNITS:
                            group = u // 8
                            if u % 8 == 0 and group >= 2:
                                act.wait_ge(pe_pv, pvs_before[a] + group - 1)
                            if a == 0 and u == 14:
                                act.wait_ge(y_out, 16)
                            take_turned((a, "P", u, 0), pt[:, group % 2, u % 8, 0:4, :])
                        if s < UNITS:
                            act.wait_ge(v_low, v_low_before[a] + s + 1)
                            act.activation(probs[:, s % PROBS, :], probs[:, s % PROBS, :], ACT.Exp, scale=-1.0,
                                           bias=low_units[:, s % PROBS:s % PROBS + 1],
                                           accum_out=sums[:, s:s + 1]).then_inc(a_exp, 1)
                        if s % 16 in (6 if a == 1 else 8, 10) and s < 48:
                            log(first + 2 * (s // 16 + 1) + (s % 16 == 10))
                        if s >= 18 and (s - 18) % 8 == 0 and s < 8 * GROUPS + 18:
                            group = (s - 18) // 8
                            act.wait_ge(pe_pv, pvs_before[a] + group + 1)
                            if group >= 1:
                                act.wait_ge(pe_turn, turn.filled((a, "O", group - 1)))
                            act.activation(o_turned[:, :], bank_o[:, :], ACT.Copy).then_inc(a_o, 1)
                        if s == LAST_STEP - 4 and meanwhile:
                            meanwhile()
                        if a and s >= 29 and (s - 29) % 16 == 0:
                            pair = (s - 29) // 16
                            if pair >= 1:
                                act.wait_ge(pe_turn, turn.filled((a, "W", pair - 1)))
                            take_turned((a, "T", pair), o_T[:, :, :].rearrange("p c n -> p (c n)"))

                act.preload_act_table_set("natural_log_exp_and_others")
                attention(0)

                act_take_xT(act, dense, 1)
                for i in range(4):
                    c, h = i // 2, i % 2
                    act_evacuate(act, dense, (1, "featT", i), featT[:, c, h * HALF:(h + 1) * HALF], ACT.Identity,
                                 bias=col("fcb", c))
                for i in range(2):
                    act_evacuate(act, dense, (1, "k", i), col_row[:, i * HALF:(i + 1) * HALF], ACT.Identity,
                                 bias=col("kb"))
                act.wait_ge(v_rowadd, 1)
                act.wait_ge(dense_free["act"], dense.nth[dense.index[(1, "k", 1)]])
                for s in range(NT + 2):
                    if s < NT:
                        if s >= PROBS:
                            act.wait_ge(pe_turn, turn.filled(("gat", s - PROBS, 1)))
                        act.activation(probs[:, s % PROBS, :], col_row[:, :], ACT.Identity,
                                       bias=row_add[:, s:s + 1]).then_inc(a_line, 1)
                    n = s - 1
                    if 0 <= n < NT:
                        act.wait_ge(v_leaky, n + 1)
                        act.activation(probs[:, n % PROBS, :], probs[:, n % PROBS, :], ACT.Exp, scale=-1.0,
                                       bias=low2[:, n:n + 1], accum_out=sums[:, n:n + 1]).then_inc(a_exp, 1)
                    n = s - 2
                    if n >= 0:
                        if n >= 2:
                            act.wait_ge(pe_pv, GROUPS + n - 1)
                        take_turned(("gat", n, 0), gat_pt[:, n % 2, 0:4, :])

                act_take_xT(act, dense, 2, "g1", "b1")
                log(2 * NT)
                act_take_qk(act, dense, 1, 0)
                log(2 * NT + 1)
                attention(1)
                act_take_xT(act, dense, "ffn", "g2", "b2")
                for i in range(2 * FC):
                    f, h = i // 2, i % 2
                    act_evacuate(act, dense, ("ffn", "up", i), act_up[:, f, h * HALF:(h + 1) * HALF], ACT.Gelu,
                                 bias=col("bf1", f))

                act.preload_act_table_set("natural_log_exp_and_others")
                act_take_xT(act, dense, 3)
                act_take_qk(act, dense, 2, 8)
                log(3 * NT)
                log(3 * NT + 1)
                attention(2, lambda: act_layer0_start(act, in_loop))
                act_layer0_end(act, in_loop)

            @block.vector
            def _(dve):
                own = Own(dve)
                link = own.link

                def biased(a, u):
                    p, g, n, h, tile = unit(u)
                    dve.wait_ge(pe_scores, a * UNITS + u + 1)
                    if g == 0 and u % 16 in (0, 4):
                        i = STACK[a] * NT + tile
                        if a == 2:
                            dve.wait_ge(a_ln, 2 * NT - 2 + tile + 1)
                        elif i >= 2:
                            dve.wait_ge(p_bias, i - 1)
                    if u >= PROBS:
                        dve.wait_ge(pe_turn, turn.filled((a, "P", u - PROBS, 1)))
                    dve.tensor_tensor_reduce(probs[:, u % PROBS, :], bank_sc[:, 2 * (u % 2):2 * (u % 2) + 2, :],
                                             ring_adj[:, tile % 4, :], -1.0, BIG, ALU.add, ALU.min,
                                             low_units[:, u % PROBS:u % PROBS + 1]).then_inc(v_low, 1)

                def finish(a, group):
                    g, p = group % 2, group // 2
                    of_group = slice(8 * group, 8 * group + 8)
                    if group >= 1:
                        dve.wait_ge(turn_free["dve"], turn.nth[turn.index[(a, "O", group - 1)]])
                    dve.wait_ge(a_exp, exps_before[a] + 8 * group + 8)
                    link(dve.reciprocal(recip, sums[:, of_group]))
                    key = (a, "O", group)
                    dve.wait_ge(pe_turn, turn.filled(key))
                    ins = dve.tensor_tensor(
                        o_nat[:, :, g * P:(g + 1) * P].rearrange("p n (j d) -> p n j d", j=HG),
                        bank_tr[:, turn.bank(key), 0:2 * P].rearrange("p (n j d) -> p n j d", n=2, j=HG),
                        recip.rearrange("p (n j) -> p n j", n=2).unsqueeze(3).to_broadcast([P, 2, HG, HD]), ALU.mult)
                    ins.then_inc(turn_free["dve"], 1)
                    if a == 0:
                        if group == 0:
                            dve.wait_ge(x_res_in, 16)
                        dve.wait_ge(turn_free["dve"], turn.nth[turn.index[key]])
                        xs = x_sb[:, 2 * p:2 * p + 2, g * P:(g + 1) * P]
                        dve.tensor_tensor(xs, xs, o_nat[:, :, g * P:(g + 1) * P], ALU.add).then_inc(v_x, 1)

                def project_out(a, pair):
                    key = (a, "W", pair)
                    xs = x_sb[:, 2 * pair:2 * pair + 2, :]
                    if pair:
                        row_stats(range(2 * pair - 2, 2 * pair))
                    link(dve.tensor_tensor(xs, xs, rows[:, R_BO[a]:R_BO[a] + 1, :].to_broadcast([P, 2, D]), ALU.add))
                    dve.wait_ge(pe_turn, turn.filled(key))
                    dve.tensor_tensor(xs, xs, bank_tr[:, turn.bank(key), :].rearrange("p (n d) -> p n d", n=2),
                                      ALU.add).then_inc(turn_free["dve"], 1)
                    dve.wait_ge(turn_free["dve"], turn.nth[turn.index[key]])
                    dve.sem_inc(v_x, 1)

                def take_turned(key, dst):
                    dve.wait_ge(pe_turn, turn.filled(key))
                    dve.tensor_copy(dst, bank_tr[:, turn.bank(key), :].rearrange("p (m n) -> p m n", n=P)
                                    ).then_inc(turn_free["dve"], 1)

                def attention(a, meanwhile=None):
                    for s in range(LAST_STEP + 1):
                        if s < UNITS:
                            biased(a, s)
                        u = s - LAG
                        if 0 <= u < UNITS:
                            group = u // 8
                            if u % 8 == 0 and group >= 2:
                                dve.wait_ge(pe_pv, pvs_before[a] + group - 1)
                            if a == 0 and u == 14:
                                dve.wait_ge(y_out, 16)
                            take_turned((a, "P", u, 1), pt[:, group % 2, u % 8, 4:8, :])
                        if s == LAST_STEP - 4 and meanwhile:
                            meanwhile()
                        if s >= 20 and (s - 20) % 8 == 0:
                            finish(a, (s - 20) // 8)
                        if a and s >= 30 and (s - 30) % 16 == 0:
                            project_out(a, (s - 30) // 16)

                def row_stats(tiles):
                    for i in tiles:
                        own.mark(dve.bn_stats(stats[:, i, :], x_sb[:, i, :]))
                    own.wait()
                    for i in tiles:
                        own.mark(dve.bn_aggr(mean_var[:, i, :], stats[:, i, :]))

                def norm(n, rest):
                    row_stats(rest)
                    own.wait()
                    dve.tensor_scalar(var_eps, mean_var[:, :, 1], LN_EPS, None, ALU.add).then_inc(v_stats, 1)
                    dve.wait_ge(p_rstd, n + 1)
                    if n == 2:
                        for i in range(NT):
                            own.mark(dve.scalar_tensor_tensor(out=y_sb[:, i, :], in0=x_sb[:, i, :],
                                                              scalar=mean_var[:, i, 0:1], in1=rows[:, R_GAMMA, :],
                                                              op0=ALU.subtract, op1=ALU.mult))
                        own.wait()
                        for i in range(NT):
                            dve.scalar_tensor_tensor(out=y_sb[:, i, :], in0=y_sb[:, i, :], scalar=rstd[:, i:i + 1],
                                                     in1=rows[:, R_BETA, :], op0=ALU.mult, op1=ALU.add
                                                     ).then_inc(v_normed, 1)
                        return
                    for i in range(NT):
                        dve.tensor_scalar(normed[:, i, :], x_sb[:, i, :], mean_var[:, i, 0:1], rstd[:, i:i + 1],
                                          ALU.subtract, ALU.mult).then_inc(v_normed, 1)
                    dve.wait_ge(v_normed, (n + 1) * NT)

                attention(0)

                dve.wait_ge(v_x, X_DONE[0])
                dve_take_xT(dve, dense, 1)
                for i in range(4):
                    dve_take_rows(dve, dense, (1, "feat", i), i, R_FCB)
                dve.wait_ge(dense_free["dve"], dense.nth[dense.index[(1, "feat", 3)]])
                dve_row_sums(dve, own, v_sb, R_QW, col("qb"))
                for s in range(NT + 5):
                    if s < NT:
                        buf = probs[:, s % PROBS, :]
                        dve.wait_ge(a_line, s + 1)
                        dve.wait_ge(p_bias, NT + s - 1)
                        dve.tensor_tensor_reduce(buf, buf, ring_adj[:, s % 4, :], -1.0, BIG, ALU.add, ALU.min,
                                                 low[:, s:s + 1]).then_inc(v_low, 1)
                        dve.wait_ge(v_low, UNITS + s + 1)
                        link(dve.scalar_tensor_tensor(out=low2[:, s:s + 1], in0=low[:, s:s + 1], scalar=LEAK,
                                                      in1=low[:, s:s + 1], op0=ALU.mult, op1=ALU.min))
                        dve.scalar_tensor_tensor(out=buf, in0=buf, scalar=LEAK, in1=buf, op0=ALU.mult, op1=ALU.min
                                                 ).then_inc(v_leaky, 1)
                    n = s - 2
                    if 0 <= n < NT:
                        if n >= 2:
                            dve.wait_ge(pe_pv, GROUPS + n - 1)
                        take_turned(("gat", n, 1), gat_pt[:, n % 2, 4:8, :])
                    n = s - 4
                    if 0 <= n < NT:
                        dve.wait_ge(a_exp, UNITS + n + 1)
                        link(dve.reciprocal(recip[:, n:n + 1], sums[:, n:n + 1]))
                        dve.wait_ge(pe_pv, GROUPS + n + 1)
                        dve.scalar_tensor_tensor(out=x_sb[:, n, :], in0=bank_sc[:, n % 4, 0:D],
                                                 scalar=recip[:, n:n + 1], in1=x_sb[:, n, :], op0=ALU.mult,
                                                 op1=ALU.add).then_inc(v_x, 1)
                    if 1 <= n <= NT:
                        dve.wait_ge(v_x, X_DONE[0] + n)
                        row_stats([n - 1])

                norm(0, [])
                dve_split_qk(dve, own, dense, 1)
                for i in range(4):
                    dve_take_rows(dve, dense, (2, "v", i), i, R_BV[1])
                attention(1)
                norm(1, (NT - 2, NT - 1))
                for i in range(4):
                    xs = x_sb[:, 2 * i:2 * i + 2, :]
                    link(dve.tensor_tensor(xs, xs, rows[:, R_BF2:R_BF2 + 1, :].to_broadcast([P, 2, D]), ALU.add))
                    dve.wait_ge(pe_dense, dense.filled(("ffn", "down", i)))
                    dve.tensor_tensor(xs, xs, bank_sc[:, dense.bank(("ffn", "down", i)), :].rearrange(
                        "p (n d) -> p n d", n=2), ALU.add).then_inc(dense_free["dve"], 1)
                    dve.wait_ge(dense_free["dve"], dense.nth[dense.index[("ffn", "down", i)]])
                    dve.sem_inc(v_x, 1)

                dve_take_xT(dve, dense, 3)
                dve_split_qk(dve, own, dense, 2)
                for i in range(4):
                    dve_take_rows(dve, dense, (3, "v", i), i, R_BV[2])
                attention(2, lambda: dve_layer0_start(dve, own, in_loop))
                norm(2, (NT - 2, NT - 1))
                dve_layer0_end(dve, own, in_loop)

        clear_semaphores()
    nc.sync.wait_ge(y_out, 16)
    nc.sync.wait_ge(x_res_in, 16)
    nc.sync.wait_ge(late_cat, 16 * STACK_DMAS)
    ctx.close()


INPUTS = ["x", "adj", "L0_gnn_W_q", "L0_gnn_b_q", "L0_gnn_W_k", "L0_gnn_b_k", "L0_gnn_W_v", "L0_gnn_b_v",
          "L0_gnn_w_g", "L0_gnn_b_g", "L1_gnn_fc_w", "L1_gnn_fc_b", "L1_gnn_q_w", "L1_gnn_q_b", "L1_gnn_k_w",
          "L1_gnn_k_b", "L2_gnn_Wq", "L2_gnn_bq", "L2_gnn_Wk", "L2_gnn_bk", "L2_gnn_Wv", "L2_gnn_bv", "L2_gnn_Wo",
          "L2_gnn_bo", "L2_gnn_g1", "L2_gnn_b1", "L2_gnn_g2", "L2_gnn_b2", "L2_gnn_Wf1", "L2_gnn_bf1", "L2_gnn_Wf2",
          "L2_gnn_bf2", "L3_gnn_Wq", "L3_gnn_bq", "L3_gnn_Wk", "L3_gnn_bk", "L3_gnn_Wv", "L3_gnn_bv", "L3_gnn_Wo",
          "L3_gnn_bo", "L3_gnn_gamma", "L3_gnn_beta"]


def kernel(**inputs):
    import numpy as _np
    import concourse.bacc as _bacc
    from concourse.bass_utils import run_bass_kernel_spmd as _run

    nc = _bacc.Bacc("TRN2", target_bir_lowering=False, num_devices=1)
    arrays, tensors = {}, {}
    for name in INPUTS:
        a = _np.ascontiguousarray(inputs[name])
        if a.ndim == 0:
            a = a.reshape(1)
        arrays[f"in_{name}"] = a
        tensors[name] = nc.dram_tensor(f"in_{name}", a.shape, mybir.dt.from_np(a.dtype), kind="ExternalInput").ap()
    tensors["out"] = nc.dram_tensor("out_0", (B, N, D), F32, kind="ExternalOutput").ap()
    graph_layers(nc, tensors)
    return _run(nc, [arrays], core_ids=[0]).results[0]["out_0"]
```

```python
from contextlib import ExitStack

import concourse.bass as bass
from concourse import mybir

P = 128
B, N, D = 8, 1024, 256
H = 8
HD = D // H
F = 4 * D
NT = N // P
DC = D // P
FC = F // P
HG = 4
UNITS = H * NT
GROUPS = UNITS // 8
PAIRS = GROUPS // 2
HALF = 512
LAG = 3
PROBS = 4
SCALE = float(HD) ** -0.5
LN_EPS = 1e-5
LOG_EPS = 1e-9
ADJ_MIN = 1e-8
NEG_INF = -1e9
LEAK = 0.01
BIG = 3.0e38
GATE_MIN = 1e-6

ALU = mybir.AluOpType
ACT = mybir.ActivationFunctionType
F32 = mybir.dt.float32
F16 = mybir.dt.float16

STACK = [0, 2, 3]
LAST_STEP = 8 * (GROUPS - 1) + 22
HALF_FREE, PRODUCTS_DONE, OUT_TURNED, PAIR_TURNED = LAST_STEP - 11, LAST_STEP - 4, LAST_STEP - 2, LAST_STEP - 1


class Ring:

    def __init__(self, banks):
        self.banks, self.index, self.owner, self.nth, self.count = banks, {}, [], [], {"act": 0, "dve": 0, "lo": 0}
        self.lo_done, self.hi_done, self.slots = {}, {}, []

    def add(self, key, owner, split=False):
        self.index[key] = len(self.owner)
        self.owner.append(owner)
        self.count[owner] += 1
        if split:
            self.lo_done[key] = len(self.lo_done) + 1
            if owner == "act":
                self.slots.append(key)
            else:
                self.hi_done[key] = self.count[owner]
        self.nth.append(self.lo_done[key] if owner == "lo" else self.count[owner])

    def bank(self, key):
        return self.index[key] % self.banks

    def filled(self, key):
        return self.index[key] + 1

    def wait_free(self, eng, key, emptied):
        k = self.index[key] - self.banks
        if k >= 0:
            eng.wait_ge(emptied[self.owner[k]], self.nth[k])


def turn_ring():
    ring = Ring(3)

    def attention(a):
        for s in range(LAST_STEP + 1):
            u = s - LAG
            if 0 <= u < UNITS:
                ring.add((a, "P", u, 0), "act")
                ring.add((a, "P", u, 1), "dve")
            if s >= 20 and (s - 20) % 8 == 0:
                ring.add((a, "O", (s - 20) // 8), "dve")
            if a and s >= 29 and (s - 29) % 16 == 0:
                ring.add((a, "T", (s - 29) // 16), "act")
            if a and s >= 30 and (s - 30) % 16 == 0:
                ring.add((a, "W", (s - 30) // 16), "dve")

    attention(0)
    for t in range(NT):
        ring.add(("gat", t, 0), "act")
        ring.add(("gat", t, 1), "dve")
    attention(1)
    attention(2)
    return ring


BY_GROUP = [(0, 0, 0), (0, 1, 0), (0, 1, 1), (0, 0, 1), (1, 0, 0), (1, 1, 0), (1, 0, 1), (1, 1, 1)]
BY_ROWS = [(0, 0, 0), (0, 1, 0), (1, 0, 0), (1, 1, 0), (0, 1, 1), (0, 0, 1), (1, 0, 1), (1, 1, 1)]
QK = {0: BY_GROUP, 2: BY_ROWS, 3: BY_ROWS}
UP = [(f, h) for h in range(2) for f in range(FC)]
XT_AT = FC


def projections(ring, layer):
    def x_half(h):
        for i in (2 * h, 2 * h + 1):
            ring.add((layer, "xT", i), "act" if layer == 2 else "lo", split=True)

    x_half(0)
    if layer == 0:
        x_half(1)
    if layer == 3:
        ring.add(("ffn", "down", 3), "dve")
    for i in range(8):
        if layer and i == 2:
            x_half(1)
        if layer == 0 and i == 4:
            for c in range(2):
                ring.add((0, "c", c), "act")
        ring.add((layer, "qk", i), "act", split=True)
    for i in range(4):
        ring.add((layer, "v", i), "dve")


def first_ring():
    ring = Ring(4)
    projections(ring, 0)
    return ring


def dense_ring():
    ring = Ring(4)
    for h in range(2):
        for i in (2 * h, 2 * h + 1):
            ring.add((1, "xT", i), "lo", split=True)
        if h == 0:
            for i in range(2):
                ring.add((1, "feat", i), "dve")
        for c in range(DC):
            ring.add((1, "featT", c, h), "act")
    for i in range(2):
        ring.add((1, "k", i), "act")
    for i in (2, 3):
        ring.add((1, "feat", i), "dve")
    projections(ring, 2)
    for i in (0, 1):
        ring.add(("ffn", "xT", i), "act", split=True)
    for i in range(2 * FC):
        if i == XT_AT:
            for x in (2, 3):
                ring.add(("ffn", "xT", x), "act", split=True)
            ring.add(("ffn", "down", 0), "dve")
        ring.add(("ffn", "up", i), "act", split=True)
    for i in (1, 2):
        ring.add(("ffn", "down", i), "dve")
    projections(ring, 3)
    projections(ring, 0)
    return ring


COLS = {}
_at = 0
for _name, _n in (("bq0", DC), ("bk0", DC), ("bq1", DC), ("bk1", DC), ("bq2", DC), ("bk2", DC), ("g1", DC),
                  ("b1", DC), ("g2", DC), ("b2", DC), ("bf1", FC), ("fcb", DC), ("kw", DC), ("wgc", DC),
                  ("bg", 1), ("qb", 1), ("kb", 1), ("sbq0", DC), ("sbq1", DC), ("sbq2", DC),
                  ("log_eps", 1), ("minus_half", NT)):
    COLS[_name] = _at
    _at += _n
NCOLS = _at


def graph_layers(nc, t):
    ctx = ExitStack()

    def sb(name, shape, dt=F32):
        return ctx.enter_context(nc.sbuf_tensor(name, shape, dt))

    def sem(name):
        return ctx.enter_context(nc.semaphore(name))

    ident = sb("ident", [P, P])
    vec = sb("vec", [P, NCOLS])
    w_qkv = [sb(f"w_qkv{a}", [P, 3, 2, DC, D], F16) for a in range(3)]
    w_o = [None] + [sb(f"w_o{a}", [P, DC, D]) for a in (1, 2)]
    w_fc = sb("w_fc", [P, 2, DC, D], F16)
    w_up = sb("w_up", [P, 2, DC, F], F16)
    w_down = sb("w_down", [P, 2, FC, D], F16)
    rows = sb("rows", [P, 11, D])
    R_BV, R_BO, R_BF2, R_GAMMA, R_BETA, R_WGA, R_FCB, R_QW = (0, 1, 2), (None, 3, 4), 5, 6, 7, 8, 9, 10
    wide_wg = sb("wide_wg", [P, 2, DC, P], F16)
    wide_kw = sb("wide_kw", [P, DC, P])

    x_sb = sb("x_sb", [P, NT, D])
    ring_adj = sb("ring_adj", [P, 4, N])
    pt = sb("pt", [P, 2, 8, NT, P])
    probs = sb("probs", [P, PROBS, N])
    q_cat = sb("q_cat", [P, H, N], F16)
    k_cat = sb("k_cat", [P, H, N], F16)
    v_sb = sb("v_sb", [P, NT, D])
    col_row = sb("col_row", [P, N])
    small = sb("small", [P, 256])
    o_turned = sb("o_turned", [P, 2 * P])
    o_nat = sb("o_nat", [P, 2, D])
    o_T = sb("o_T", [P, DC, 2 * P])

    spill = nc.dram_tensor("spill", (2, 2, 2, P, N), F16, kind="Internal").ap()

    flat = pt[:, :, :, :, :].rearrange("p a b c d -> p (a b c d)")
    xT = flat[:, 0:DC * N].bitcast(F16).rearrange("p (s c n) -> p s c n", s=2, c=DC)
    x_next = ring_adj[:, 0:2, :].rearrange("p s (t d) -> p (s t) d", d=D)
    normed = flat[:, 2048:4096].rearrange("p (t d) -> p t d", t=NT)
    wide_slots = flat[:, 4096:6144].rearrange("p (i n) -> p i n", i=4)
    parts = flat[:, 6144:10240].bitcast(F16).rearrange("p (w s g n) -> p w s g n", w=2, s=2, g=2)
    products = flat[:, 2048:4096].rearrange("p (t d) -> p t d", t=NT)
    featT = flat[:, 10240:12288].rearrange("p (c n) -> p c n", c=DC)
    gat_pt = flat[:, 12288:14336].rearrange("p (b m n) -> p b m n", b=2, m=NT)
    y_sb = flat[:, 14336:16384].rearrange("p (t d) -> p t d", t=NT)
    act_up = flat[:, 8192:16384].bitcast(F16).rearrange("p (s f n) -> p s f n", s=2, f=FC)

    sums, q_sums = small[:, 0:64], small[:, 64:72]
    low, low2 = small[:, 128:136], small[:, 136:144]
    recip = small[:, 144:152]
    row_add = small[:, 152:160]
    stats = small[:, 160:208].rearrange("p (t s) -> p t s", t=NT)
    mean_var = small[:, 208:224].rearrange("p (t s) -> p t s", t=NT)
    var_eps, rstd = small[:, 224:232], small[:, 232:240]
    low_units = sb("low_units", [P, PROBS])

    bank_sc = ctx.enter_context(nc.psum_tensor("bank_sc", [P, 4, HALF], F32))
    bank_tr = ctx.enter_context(nc.psum_tensor("bank_tr", [P, 3, HALF], F32))
    bank_o = ctx.enter_context(nc.psum_tensor("bank_o", [P, 2 * P], F32))

    def col(name, c=0):
        return vec[:, COLS[name] + c:COLS[name] + c + 1]

    x_in, x_res_in = sem("x_in"), sem("x_res_in")

    def x_of(item):
        return t["x"][item].rearrange("o (t p) d -> p (o t) d", p=P)

    raw = flat.rearrange("p (w c n) -> p w c n", c=DC, n=D)
    turned = [(t["L1_gnn_fc_w"], [w_fc[:, s] for s in range(2)])]
    turned += [(t["L3_gnn_W" + n], [w_qkv[2][:, i, s] for s in range(2)]) for i, n in enumerate("qkv")]
    turned += [(t["L3_gnn_Wo"], [w_o[2][:, :, :]])]
    straight, at = [], 0
    for w, parts_of in ([(t["L0_gnn_W_" + n], [w_qkv[0][:, i, s] for s in range(2)]) for i, n in enumerate("qkv")]
                        + [(t["L2_gnn_W" + n], [w_qkv[1][:, i, s] for s in range(2)]) for i, n in enumerate("qkv")]
                        + [(t["L2_gnn_Wf1"], [w_up[:, s] for s in range(2)]),
                           (t["L2_gnn_Wf2"], [w_down[:, s] for s in range(2)])]):
        rows_, width = w.shape
        size = rows_ // P * width
        start = len(turned) * DC * D + at
        straight.append((w, flat[:, start:start + size].rearrange("p (c n) -> p c n", n=width), parts_of))
        at += size
    w_hi, w_lo = sem("w_hi"), sem("w_lo")
    by_dve = 6
    w_in, id_zero, id_ready, w_turned, w_copied, consts = (sem("w_in"), sem("id_zero"), sem("id_ready"),
                                                           sem("w_turned"), sem("w_copied"), sem("consts"))
    chunks = lambda ap: ap.rearrange("(c p) n -> p c n", p=P)
    columns = [("bq0", "L0_gnn_b_q"), ("bk0", "L0_gnn_b_k"), ("bq1", "L2_gnn_bq"), ("bk1", "L2_gnn_bk"),
               ("bq2", "L3_gnn_bq"), ("bk2", "L3_gnn_bk"), ("g1", "L2_gnn_g1"), ("b1", "L2_gnn_b1"),
               ("g2", "L2_gnn_g2"), ("b2", "L2_gnn_b2"), ("bf1", "L2_gnn_bf1"), ("fcb", "L1_gnn_fc_b")]
    on_rows = [(R_BV[0], "L0_gnn_b_v"), (R_BV[1], "L2_gnn_bv"), (R_BV[2], "L3_gnn_bv"), (R_BO[1], "L2_gnn_bo"),
               (R_BO[2], "L3_gnn_bo"), (R_BF2, "L2_gnn_bf2"), (R_GAMMA, "L3_gnn_gamma"), (R_BETA, "L3_gnn_beta"),
               (R_FCB, "L1_gnn_fc_b")]
    loads = [(raw[:, i], chunks(w)) for i, (w, _) in enumerate(turned)]
    loads += [(staged, chunks(w)) for w, staged, _ in straight]
    loads += [(w_o[1][:, :, :], chunks(t["L2_gnn_Wo"]))]
    for name, source in columns:
        n = t[source].shape[0] // P
        loads.append((vec[:, COLS[name]:COLS[name] + n], t[source].rearrange("(c p) -> p c", p=P)))
    loads.append((vec[:, COLS["kw"]:COLS["kw"] + DC], t["L1_gnn_k_w"].rearrange("a (c p) -> p (a c)", p=P)))
    loads.append((vec[:, COLS["wgc"]:COLS["wgc"] + DC], t["L0_gnn_w_g"][D:2 * D].rearrange("(c p) -> p c", p=P)))
    loads += [(rows[:, r], t[source].partition_broadcast(P)) for r, source in on_rows]
    loads += [(rows[:, R_WGA], t["L0_gnn_w_g"][0:D].partition_broadcast(P)),
              (rows[:, R_QW], t["L1_gnn_q_w"].rearrange("a d -> (a d)").partition_broadcast(P)),
              (col("bg"), t["L0_gnn_b_g"].partition_broadcast(P)), (col("qb"), t["L1_gnn_q_b"].partition_broadcast(P)),
              (col("kb"), t["L1_gnn_k_b"].partition_broadcast(P))]

    with nc.allow_non_contiguous_dma(reason="small vectors, once"), nc.Block() as block:
        @block.sync
        def _(sp):
            for dst, src in loads:
                sp.dma_start(dst, src).then_inc(w_in, 16)
            sp.dma_start(x_next, x_of(slice(0, 1))).then_inc(x_in, 16)
            sp.dma_start(x_sb[:, :, :], x_of(slice(0, 1))).then_inc(x_res_in, 16)
            sp.wait_ge(w_in, 16 * len(loads))

        @block.gpsimd
        def _(pool):
            pool.memset(ident[:, :], 0.0).then_inc(id_zero, 1)
            pool.wait_ge(id_zero, 1)
            pool.affine_select(out=ident[:, :], in_=ident[:, :], compare_op=ALU.not_equal, fill=1.0, base=0,
                               pattern=[[-1, P]], channel_multiplier=1).then_inc(id_ready, 1)
            for i, (_, staged, (hi, lo)) in enumerate(straight[by_dve:]):
                pool.wait_ge(w_hi, by_dve + i + 1)
                pool.tensor_tensor(lo, staged, hi, ALU.subtract).then_inc(w_lo, 1)
            pool.wait_ge(w_lo, len(straight) - by_dve)

        @block.tensor
        def _(pe):
            pe.wait_ge(id_ready, 1)
            pe.wait_ge(w_in, 16 * len(loads))
            for i in range(len(turned)):
                if i >= 4:
                    pe.wait_ge(w_copied, i - 3)
                for ci in range(DC):
                    for co in range(DC):
                        last = pe.transpose(bank_sc[:, i % 4, (ci * DC + co) * P:(ci * DC + co + 1) * P],
                                            raw[:, i, co, ci * P:(ci + 1) * P], ident[:, :])
                last.then_inc(w_turned, 1)

        @block.scalar
        def _(act):
            act.wait_ge(w_in, 16 * len(loads))
            for _, staged, (hi, _) in straight:
                act.activation(hi, staged, ACT.Copy).then_inc(w_hi, 1)

        @block.vector
        def _(dve):
            dve.wait_ge(w_in, 16 * len(loads))
            for a in range(3):
                dve.tensor_scalar(vec[:, COLS[f"sbq{a}"]:COLS[f"sbq{a}"] + DC],
                                  vec[:, COLS[f"bq{a}"]:COLS[f"bq{a}"] + DC], SCALE, None, ALU.mult).then_inc(consts, 1)
            dve.memset(col("log_eps"), LOG_EPS).then_inc(consts, 1)
            dve.memset(vec[:, COLS["minus_half"]:COLS["minus_half"] + NT], -0.5).then_inc(consts, 1)
            for c in range(DC):
                dve.tensor_copy(wide_kw[:, c], col("kw", c).to_broadcast([P, P])).then_inc(consts, 1)
                dve.tensor_copy(wide_wg[:, 0, c], col("wgc", c).to_broadcast([P, P])).then_inc(consts, 1)
            dve.wait_ge(consts, 5 + 2 * DC)
            for c in range(DC):
                dve.tensor_tensor(wide_wg[:, 1, c], col("wgc", c).to_broadcast([P, P]), wide_wg[:, 0, c],
                                  ALU.subtract).then_inc(consts, 1)
            for i, (_, dst) in enumerate(turned):
                dve.wait_ge(w_turned, i + 1)
                src = bank_sc[:, i % 4, :].rearrange("p (c n) -> p c n", c=DC)
                if len(dst) == 2:
                    dve.tensor_copy(dst[0], src).then_inc(consts, 1)
                    dve.wait_ge(consts, 5 + 3 * DC + i + 1)
                    dve.tensor_tensor(dst[1], src, dst[0], ALU.subtract).then_inc(w_copied, 1)
                else:
                    dve.tensor_copy(dst[0], src).then_inc(w_copied, 1)
            for i, (_, staged, (hi, lo)) in enumerate(straight[:by_dve]):
                dve.wait_ge(w_hi, i + 1)
                dve.tensor_tensor(lo, staged, hi, ALU.subtract).then_inc(w_copied, 1)
            dve.wait_ge(w_copied, len(turned) + by_dve)
            dve.wait_ge(consts, 5 + 3 * DC + len(turned) - 1)

    turn, dense = turn_ring(), dense_ring()
    parts_out = [sem("q_parts_out"), sem("k_parts_out")]
    adj_in = [sem(f"adj_in{i}") for i in range(4)]
    cat_in = [sem(f"cat_in{g}") for g in range(2)]
    y_out = sem("y_out")
    pe_dense, pe_scores, pe_turn, pe_pv = sem("pe_dense"), sem("pe_scores"), sem("pe_turn"), sem("pe_pv")
    dense_free = {"act": sem("dense_free_act"), "dve": sem("dense_free_dve")}
    turn_free = {"act": sem("turn_free_act"), "dve": sem("turn_free_dve")}
    a_hi, v_bias, v_centred = sem("a_hi"), sem("v_bias"), sem("v_centred")
    v_low, v_lo, v_x, v_rowadd, v_own = (sem("v_low"), sem("v_lo"), sem("v_x"),
                                                    sem("v_rowadd"), sem("v_own"))
    dense_free["lo"] = v_lo
    v_stats, v_normed, v_leaky = sem("v_stats"), sem("v_normed"), sem("v_leaky")
    a_exp, a_ln, a_o, a_line = sem("a_exp"), sem("a_ln"), sem("a_o"), sem("a_line")
    p_gate = sem("p_gate")
    p_clip, p_own, p_bias, p_rstd = sem("p_clip"), sem("p_own"), sem("p_bias"), sem("p_rstd")
    batch_sems = [v_bias, v_centred, p_gate, *parts_out, x_in, *adj_in, *cat_in, pe_dense, pe_scores, pe_turn, pe_pv,
                  dense_free["act"], dense_free["dve"],
                  *turn_free.values(), a_hi, v_low, v_lo, v_x, v_rowadd, v_own, v_stats, v_normed, v_leaky,
                  a_exp, a_ln, a_o, a_line, p_clip, p_own, p_bias, p_rstd]

    late_cat = sem("late_cat")

    X_DONE = [GROUPS, GROUPS + NT, GROUPS + NT + PAIRS, GROUPS + NT + 2 * PAIRS, GROUPS + NT + 3 * PAIRS]
    exps_before = [0, UNITS + NT, 2 * UNITS + NT]
    v_low_before = exps_before
    pvs_before = [0, GROUPS + NT, 2 * GROUPS + NT]

    def unit(u):
        p, g, n, j = u // 16, u // 8 % 2, u // 4 % 2, u % 4
        return p, g, n, HG * g + j, 2 * p + n

    def turned_by(a, group, owner):
        return max(turn.nth[turn.index[(a, "P", u, i)]] for u in range(8 * group, 8 * group + 8) for i in range(2)
                   if turn.owner[turn.index[(a, "P", u, i)]] == owner)

    class Stage:

        def __init__(self, ring, stacks, rowadd, adj, ln):
            self.ring, self.stacks, self.rowadd, self.adj, self.ln = ring, stacks, rowadd, adj, ln

    before_loop = Stage(first_ring(), stacks=0, rowadd=0, adj=0, ln=0)
    in_loop = Stage(dense, stacks=2, rowadd=2, adj=NT - 1, ln=3 * NT - 2)

    def gat_bank(n):
        return (dense.index[(2, "xT", 0)] + n) % 4

    def sp_load_adj(sp, item, i):
        sp.dma_start(ring_adj[:, i % 4, :], t["adj"][item, (i % NT) * P:(i % NT + 1) * P, :].rearrange(
            "o p m -> p (o m)")).then_inc(adj_in[i % 4], 16)

    def sp_stack_parts(sp, ring, layer, stacks, done):
        count = [3 * stacks, 3 * stacks]

        def out(w, g, halves):
            sp.wait_ge(v_lo, max(ring.lo_done[layer, "qk", QK[layer].index((g, w, h))] for h in halves))
            n = slice(halves[0] * HALF, (halves[-1] + 1) * HALF)
            sp.dma_start(spill[w, g][:, :, n].rearrange("s p n -> p s n"), parts[:, w, :, g, n]
                         ).then_inc(parts_out[w], 16)
            count[w] += 1

        def back(w, g, halves, signal):
            cat, order = ((q_cat, (0, 0, 1, 1)), (k_cat, (0, 1, 0, 1)))[w]
            n = slice(halves[0] * HALF, (halves[-1] + 1) * HALF)
            sp.wait_ge(parts_out[w], 16 * count[w])
            for r, part in enumerate(order):
                sp.dma_start(cat[32 * r:32 * r + 32, HG * g:HG * g + HG, n],
                             spill[w, g, part][:, n].rearrange("(j d) n -> d j n", j=HG)).then_inc(signal, 16)

        out(0, 0, (0,))
        out(1, 0, (0,))
        back(0, 0, (0,), done[0])
        back(1, 0, (0,), done[0])
        out(1, 0, (1,))
        back(1, 0, (1,), done[0])
        out(0, 0, (1,))
        back(0, 0, (1,), done[1])
        for w in range(2):
            out(w, 1, (0, 1))
        for w in range(2):
            back(w, 1, (0, 1), done[1])

    STACK_DMAS = 12

    def sp_layer0(sp, item, st):
        sp_load_adj(sp, item, 2)
        sp_load_adj(sp, item, 3)
        sp.wait_ge(pe_dense, st.ring.filled((0, "xT", 3)))
        sp.wait_ge(v_rowadd, st.rowadd + 1)
        sp_load_adj(sp, item, 0)
        sp_load_adj(sp, item, 1)
        sp_stack_parts(sp, st.ring, 0, st.stacks, (cat_in[0], late_cat))

    def sp_layer0_end(sp, st):
        for i in range(4):
            sp.wait_ge(adj_in[i], 16 * (st.adj + 1))
        sp.wait_ge(cat_in[0], 16 * STACK_DMAS * (st.stacks + 1))

    def pool_soul_bias(pool, n):
        tile = ring_adj[:, n % 4, :]
        pool.wait_ge(a_ln, n - 1)
        pool.tensor_tensor(tile, tile, col_row[:, :], ALU.add).then_inc(p_own, 1)
        pool.wait_ge(p_own, n - 1)
        pool.tensor_scalar(tile, tile, row_add[:, n:n + 1], None, ALU.add).then_inc(p_bias, 1)

    def pe_bank(pe, ring, key):
        ring.wait_free(pe, key, dense_free)
        return bank_sc[:, ring.bank(key), :]

    def pe_turn_x(pe, ring, layer, src, h):
        for i in (2 * h, 2 * h + 1):
            out = pe_bank(pe, ring, (layer, "xT", i))
            for q in range(4):
                last = pe.transpose(out[:, q * P:(q + 1) * P],
                                    src[:, 4 * (i // 2) + q, (i % 2) * P:(i % 2 + 1) * P], ident[:, :])
            last.then_inc(pe_dense, 1)

    TERMS = ((0, 0), (0, 1), (1, 0))

    def pe_xT_there(pe, ring, layer, h):
        pe.wait_ge(v_lo, ring.lo_done[layer, "xT", 2 * h + 1])

    def pe_accumulate(pe, out, lhs, rhs, chunks):
        steps = [(c, l, r) for c in range(chunks) for l, r in TERMS]
        for k, (c, l, r) in enumerate(steps):
            last = pe.matmul(out, lhs(l, c), rhs(r, c), start=(k == 0), stop=(k == len(steps) - 1))
        return last

    def pe_product(pe, ring, key, lhs, rhs, chunks=DC):
        pe_accumulate(pe, pe_bank(pe, ring, key), lhs, rhs, chunks).then_inc(pe_dense, 1)

    def pe_rows_product(pe, ring, key, lhs, rhs, chunks=DC):
        out = pe_bank(pe, ring, key)
        for n in range(2):
            last = pe_accumulate(pe, out[:, n * D:(n + 1) * D], lambda s, c: lhs(n, s, c), rhs, chunks)
        last.then_inc(pe_dense, 1)

    def pe_qk(pe, ring, a, pieces):
        layer, w = STACK[a], w_qkv[a]
        for i in pieces:
            g, m, h = QK[layer][i]
            pe_product(pe, ring, (layer, "qk", i), lambda s, c: w[:, m, s, c, g * P:(g + 1) * P],
                       lambda s, c: xT[:, s, c, h * HALF:(h + 1) * HALF])

    def pe_v(pe, ring, a):
        for i in range(4):
            pe_rows_product(pe, ring, (STACK[a], "v", i),
                            lambda n, s, c: xT[:, s, c, (2 * i + n) * P:(2 * i + n + 1) * P],
                            lambda s, c: w_qkv[a][:, 2, s, c, :])

    def pe_layer0_turn_x(pe, st):
        pe.wait_ge(x_in, 16)
        for h in range(2):
            pe_turn_x(pe, st.ring, 0, x_next, h)

    def pe_layer0_qk(pe, st, pieces):
        for h in range(2):
            pe_xT_there(pe, st.ring, 0, h)
        pe_qk(pe, st.ring, 0, pieces)

    def pe_layer0_end(pe, st):
        for i in range(2):
            pe_product(pe, st.ring, (0, "c", i), lambda s, c: wide_wg[:, s, c, :],
                       lambda s, c: xT[:, s, c, i * HALF:(i + 1) * HALF])
        pe_qk(pe, st.ring, 0, range(4, 8))
        pe_v(pe, st.ring, 0)

    def act_evacuate(act, ring, key, dst, func=ACT.Copy, **kw):
        act.wait_ge(pe_dense, ring.filled(key))
        act.activation(dst, bank_sc[:, ring.bank(key), :], func, **kw).then_inc(dense_free["act"], 1)

    def act_split(act, ring, key, hi, func=ACT.Copy, **kw):
        if key in ring.hi_done:
            act.wait_ge(pe_dense, ring.filled(key))
            act.activation(hi, bank_sc[:, ring.bank(key), :], func, **kw).then_inc(a_hi, 1)
            return
        k = ring.slots.index(key)
        if k >= 4:
            act.wait_ge(v_lo, ring.lo_done[ring.slots[k - 4]])
        act.wait_ge(pe_dense, ring.filled(key))
        act.activation(hi, bank_sc[:, ring.bank(key), :], func, **kw)
        act.activation(wide_slots[:, k % 4, :], bank_sc[:, ring.bank(key), :], func, **kw
                       ).then_inc(dense_free["act"], 1)

    def xT_half(i, part):
        return xT[:, part, i % 2, (i // 2) * HALF:(i // 2 + 1) * HALF]

    def qk_half(layer, i, part):
        g, m, h = QK[layer][i]
        return parts[:, m, part, g, h * HALF:(h + 1) * HALF]

    def act_take_xT(act, ring, layer, h, gain=None, shift=None):
        for i in (2 * h, 2 * h + 1):
            if gain is None:
                act_split(act, ring, (layer, "xT", i), xT_half(i, 0))
            else:
                act_split(act, ring, (layer, "xT", i), xT_half(i, 0), ACT.Identity, bias=col(shift, i % 2),
                          scale=col(gain, i % 2))

    def act_take_qk(act, ring, a, pieces):
        for i in pieces:
            g, m, _ = QK[STACK[a]][i]
            bias = col(f"bk{a}", g) if m else col(f"sbq{a}", g)
            act_split(act, ring, (STACK[a], "qk", i), qk_half(STACK[a], i, 0), ACT.Identity, bias=bias,
                      scale=1.0 if m else SCALE)

    def act_layer0_xT(act, st):
        for h in range(2):
            act_take_xT(act, st.ring, 0, h)

    def act_layer0_end(act, st):
        for i in range(2):
            act_evacuate(act, st.ring, (0, "c", i), col_row[:, i * HALF:(i + 1) * HALF])
        for n in range(2):
            act_take_qk(act, st.ring, 0, range(4 + 2 * n, 6 + 2 * n))
            act.wait_ge(adj_in[n], 16 * (st.adj + 1))
            act.activation(ring_adj[:, n, :], ring_adj[:, n, :], ACT.Ln, bias=col("log_eps")).then_inc(a_ln, 1)

    class Own:

        def __init__(self, dve):
            self.dve, self.n = dve, 0

        def mark(self, ins):
            self.n += 1
            ins.then_inc(v_own, 1)

        def wait(self):
            self.dve.wait_ge(v_own, self.n)

        def link(self, ins):
            self.mark(ins)
            self.wait()

    def dve_split(dve, ring, key, hi, lo):
        if key in ring.hi_done:
            dve.wait_ge(a_hi, ring.hi_done[key])
            whole = bank_sc[:, ring.bank(key), :]
        else:
            dve.wait_ge(dense_free["act"], ring.nth[ring.index[key]])
            whole = wide_slots[:, ring.slots.index(key) % 4, :]
        dve.tensor_tensor(lo, whole, hi, ALU.subtract).then_inc(v_lo, 1)

    def dve_split_xT(dve, ring, layer, h):
        for i in (2 * h, 2 * h + 1):
            dve_split(dve, ring, (layer, "xT", i), xT_half(i, 0), xT_half(i, 1))

    def dve_row_sums(dve, own, src, r, tiles, out):
        for n in tiles:
            own.mark(dve.tensor_tensor_reduce(products[:, n, :], src[:, n, :], rows[:, r, :], 1.0, 0.0, ALU.mult,
                                              ALU.add, out[:, n:n + 1]))

    def dve_row_add(dve, own, add):
        own.wait()
        dve.tensor_scalar(row_add, low, add, None, ALU.add).then_inc(v_rowadd, 1)

    def dve_split_qk(dve, ring, a, pieces):
        for i in pieces:
            dve_split(dve, ring, (STACK[a], "qk", i), *(qk_half(STACK[a], i, part) for part in range(2)))

    def dve_take_rows(dve, ring, key, i, r):
        dve.wait_ge(pe_dense, ring.filled(key))
        dve.tensor_tensor(v_sb[:, 2 * i:2 * i + 2, :],
                          bank_sc[:, ring.bank(key), :].rearrange("p (n d) -> p n d", n=2),
                          rows[:, r:r + 1, :].to_broadcast([P, 2, D]), ALU.add).then_inc(dense_free["dve"], 1)

    def dve_layer0_start(dve, own, st):
        for h in range(2):
            dve_split_xT(dve, st.ring, 0, h)
        dve.wait_ge(x_in, 16)
        dve_row_sums(dve, own, x_next, R_WGA, range(NT), low)
        dve_row_add(dve, own, col("bg"))

    def dve_layer0_end(dve, st, between):
        def soul_bias(n):
            tile = ring_adj[:, n, :]
            dve.wait_ge(a_ln, st.ln + n + 1)
            dve.scalar_tensor_tensor(out=tile, in0=tile, scalar=row_add[:, n:n + 1], in1=col_row[:, :], op0=ALU.add,
                                     op1=ALU.add).then_inc(v_bias, 1)

        for i in range(4):
            dve_split_qk(dve, st.ring, 0, (4 + i,))
            between(i)
        for i in range(4):
            dve_take_rows(dve, st.ring, (0, "v", i), i, R_BV[0])
            if i == 0:
                between(4)
            if i % 2:
                soul_bias(i // 2)
        dve.wait_ge(v_bias, 2)

    with nc.Block() as block:
        @block.sync
        def _(sp):
            sp_layer0(sp, slice(0, 1), before_loop)
            sp_layer0_end(sp, before_loop)
            sp.sem_inc(y_out, 16)

        @block.tensor
        def _(pe):
            pe_layer0_turn_x(pe, before_loop)
            pe_layer0_qk(pe, before_loop, range(4))
            pe_layer0_end(pe, before_loop)

        @block.scalar
        def _(act):
            act.preload_act_table_set("natural_log_exp_and_others")
            act_layer0_xT(act, before_loop)
            act_take_qk(act, before_loop.ring, 0, range(4))
            act_layer0_end(act, before_loop)

        @block.vector
        def _(dve):
            own = Own(dve)
            dve_layer0_start(dve, own, before_loop)
            dve_split_qk(dve, before_loop.ring, 0, range(4))
            dve_layer0_end(dve, before_loop, lambda k: None)

    def clear_semaphores():
        engines = (nc.sync, nc.scalar, nc.vector, nc.tensor)
        for i, s in enumerate(batch_sems):
            engines[i % 4].sem_clear(s)
        nc.all_engine_barrier()

    clear_semaphores()

    with nc.Fori(0, B) as b:
        next_item = bass.ds((b + 1) % B, 1)
        with nc.Block() as block:
            @block.sync
            def _(sp):
                for pair in range(1, 4 * PAIRS - 1):
                    last, q = (pair - 1) // PAIRS, (pair - 1) % PAIRS
                    if last == 1:
                        sp.wait_ge(v_low, UNITS + 2 * (q + 1))
                    else:
                        sp.wait_ge(v_low, (0, None, UNITS + NT, 2 * UNITS + NT)[last] + 16 * (q + 1))
                    sp_load_adj(sp, bass.ds(b, 1), 2 * pair + 2)
                    sp_load_adj(sp, bass.ds(b, 1), 2 * pair + 3)
                    if pair in (1, 2, 3):
                        sp.sem_clear((late_cat, y_out, x_res_in)[pair - 1])
                    if pair == 2 * PAIRS:
                        sp_stack_parts(sp, dense, 2, 0, cat_in)
                    if pair == 3 * PAIRS:
                        sp_stack_parts(sp, dense, 3, 1, cat_in)
                sp.wait_ge(v_low, 2 * UNITS + NT + 48)
                sp.dma_start(x_next, x_of(next_item)).then_inc(x_in, 16)
                sp.wait_ge(v_low, 3 * UNITS + NT)
                sp_layer0(sp, next_item, in_loop)
                sp.wait_ge(v_centred, NT)
                sp.dma_start(x_sb[:, :, :], x_of(next_item)).then_inc(x_res_in, 16)
                sp.wait_ge(v_normed, 3 * NT)
                sp.dma_start(t["out"][bass.ds(b, 1)].rearrange("o (t p) d -> p (o t) d", p=P), y_sb
                             ).then_inc(y_out, 16)
                sp_layer0_end(sp, in_loop)

            @block.gpsimd
            def _(pool):
                def clip(i):
                    tile = ring_adj[:, i % 4, :]
                    pool.wait_ge(adj_in[i % 4], 16 * (i // 4))
                    pool.tensor_scalar(tile, tile, ADJ_MIN, None, ALU.max).then_inc(p_clip, 1)

                def bias(i):
                    tile = ring_adj[:, i % 4, :]
                    if i < NT:
                        pool_soul_bias(pool, i)
                        return
                    pool.wait_ge(adj_in[i % 4], 16 * (i // 4))
                    if i < 2 * NT:
                        pool.tensor_scalar(tile, tile, 1.0, -NEG_INF, ALU.subtract, ALU.mult).then_inc(p_bias, 1)
                        return
                    k, gate = i - 2 * NT, col_row[:, :]
                    if k == 0:
                        pool.wait_ge(a_line, NT)
                    else:
                        pool.wait_ge(p_bias, i - 2)
                    pool.tensor_scalar(gate, tile, 0.75, 0.25, ALU.mult, ALU.add).then_inc(p_gate, 1)
                    pool.wait_ge(p_gate, 3 * k + 1)
                    pool.tensor_scalar(gate, gate, GATE_MIN, None, ALU.max).then_inc(p_gate, 1)
                    pool.tensor_scalar(tile, tile, 2.0, -1.0, ALU.mult, ALU.add).then_inc(p_gate, 1)
                    pool.wait_ge(p_gate, 3 * k + 3)
                    pool.wait_ge(a_ln, NT - 2 + k + 1)
                    pool.tensor_tensor(tile, tile, gate, ALU.add).then_inc(p_bias, 1)

                def reciprocal_std(nth, start, end):
                    pool.wait_ge(v_stats, nth + 1)
                    half = vec[:, COLS["minus_half"] + start:COLS["minus_half"] + end]
                    pool.tensor_tensor(rstd[:, start:end], var_eps[:, start:end], half, ALU.pow).then_inc(p_rstd, 1)

                for i in range(2, 2 * NT):
                    bias(i)
                reciprocal_std(0, 0, 4)
                reciprocal_std(1, 4, 8)
                for i in range(2 * NT, 3 * NT):
                    bias(i)
                clip(3 * NT)
                clip(3 * NT + 1)
                reciprocal_std(2, 0, 4)
                reciprocal_std(3, 4, 8)
                for i in range(3 * NT + 2, 4 * NT):
                    clip(i)
                reciprocal_std(4, 0, NT)

            @block.tensor
            def _(pe):
                def scores(a, u):
                    p, g, n, h, tile = unit(u)
                    if a == 0 and u == 8:
                        pe.wait_ge(late_cat, 16 * STACK_DMAS)
                    if a and u % 8 == 0 and u < 16:
                        pe.wait_ge(cat_in[g], 16 * STACK_DMAS * a)
                    if a and u == 0:
                        k = dense.index[(STACK[a], "qk", 7)]
                        pe.wait_ge(dense_free["act"], dense.nth[k])
                        pe.wait_ge(dense_free["dve"], dense.nth[dense.index[(STACK[a], "v", 3)]])
                    if u >= 2:
                        pe.wait_ge(v_low, v_low_before[a] + u - 1)
                    for h2 in range(2):
                        last = pe.matmul(bank_sc[:, 2 * (u % 2) + h2, :], q_cat[:, h, tile * P:(tile + 1) * P],
                                         k_cat[:, h, h2 * HALF:(h2 + 1) * HALF], start=True, stop=True)
                    last.then_inc(pe_scores, 1)

                def turn_probs(key, src, slot):
                    for i in range(2):
                        turn.wait_free(pe, (*key, i), turn_free)
                        for q in range(4):
                            last = pe.transpose(bank_tr[:, turn.bank((*key, i)), q * P:(q + 1) * P],
                                                src[:, (4 * i + q) * P:(4 * i + q + 1) * P], ident[:, :])
                        last.then_inc(pe_turn, 1)

                def attention(a, meanwhile):
                    for s in range(LAST_STEP + 1):
                        if s < UNITS:
                            scores(a, s)
                        u = s - LAG
                        if 0 <= u < UNITS:
                            pe.wait_ge(a_exp, exps_before[a] + u + 1)
                            turn_probs((a, "P", u), probs[:, u % PROBS, :], u)
                        group, m = (s - 11) // 8, (s - 11) % 8
                        tiles = [(0,), (1,), (2,), (3, 4), (5,), (6,), (7,), ()][m]
                        if 0 <= group < GROUPS:
                            if m == 0:
                                for owner in ("act", "dve"):
                                    pe.wait_ge(turn_free[owner], turned_by(a, group, owner))
                                if a * GROUPS + group >= 1:
                                    pe.wait_ge(a_o, a * GROUPS + group)
                            g = group % 2
                            for m in tiles:
                                for j in range(HG):
                                    h = HG * g + j
                                    last = pe.matmul(
                                        bank_o[32 * j:32 * j + 32, :], v_sb[:, m, h * HD:(h + 1) * HD],
                                        pt[:, group % 2, :, m, :].rearrange("p (n j) q -> p n j q", n=2)[:, :, j, :],
                                        start=(m == 0), stop=(m == NT - 1), skip_group_check=True)
                            if NT - 1 in tiles:
                                last.then_inc(pe_pv, 1)
                        if s >= 20 and (s - 20) % 8 == 0:
                            group = (s - 20) // 8
                            key = (a, "O", group)
                            pe.wait_ge(a_o, a * GROUPS + group + 1)
                            turn.wait_free(pe, key, turn_free)
                            for n in range(2):
                                last = pe.transpose(bank_tr[:, turn.bank(key), n * P:(n + 1) * P],
                                                    o_turned[:, n * P:(n + 1) * P], ident[:, :])
                            last.then_inc(pe_turn, 1)
                        if a and s >= 29 and (s - 29) % 16 == 0:
                            pair = (s - 29) // 16
                            key = (a, "T", pair)
                            k = turn.index[(a, "O", 2 * pair + 1)]
                            pe.wait_ge(turn_free["dve"], turn.nth[k])
                            turn.wait_free(pe, key, turn_free)
                            for c in range(DC):
                                for n in range(2):
                                    last = pe.transpose(bank_tr[:, turn.bank(key), (2 * c + n) * P:(2 * c + n + 1) * P],
                                                        o_nat[:, n, c * P:(c + 1) * P], ident[:, :])
                            last.then_inc(pe_turn, 1)
                        if a and s >= 30 and (s - 30) % 16 == 0:
                            pair = (s - 30) // 16
                            key = (a, "W", pair)
                            pe.wait_ge(turn_free["act"], turn.nth[turn.index[(a, "T", pair)]])
                            turn.wait_free(pe, key, turn_free)
                            for n in range(2):
                                for c in range(DC):
                                    last = pe.matmul(bank_tr[:, turn.bank(key), n * D:(n + 1) * D],
                                                     o_T[:, c, n * P:(n + 1) * P], w_o[a][:, c, :],
                                                     start=(c == 0), stop=(c == DC - 1))
                            last.then_inc(pe_turn, 1)
                        if s in meanwhile:
                            meanwhile[s]()

                def layer1_turn_x(h):
                    pe.wait_ge(v_x, GROUPS // 2 * (h + 1))
                    pe_turn_x(pe, dense, 1, x_sb, h)

                def features(tile_pairs):
                    pe_xT_there(pe, dense, 1, tile_pairs[0] // 2)
                    for i in tile_pairs:
                        pe_rows_product(pe, dense, (1, "feat", i),
                                        lambda n, s, c: xT[:, s, c, (2 * i + n) * P:(2 * i + n + 1) * P],
                                        lambda s, c: w_fc[:, s, c, :])

                def features_turned(h):
                    for c in range(DC):
                        pe_product(pe, dense, (1, "featT", c, h), lambda s, k: w_fc[:, s, k, c * P:(c + 1) * P],
                                   lambda s, k: xT[:, s, k, h * HALF:(h + 1) * HALF])

                def k_product(h):
                    pe.wait_ge(dense_free["act"], dense.nth[dense.index[(1, "featT", 1, h)]])
                    out = pe_bank(pe, dense, (1, "k", h))
                    for c in range(DC):
                        last = pe.matmul(out, wide_kw[:, c, :], featT[:, c, h * HALF:(h + 1) * HALF], start=(c == 0),
                                         stop=(c == DC - 1))
                    last.then_inc(pe_dense, 1)

                attention(0, {HALF_FREE: lambda: layer1_turn_x(0), PRODUCTS_DONE: lambda: features((0, 1)),
                              OUT_TURNED: lambda: features_turned(0)})

                layer1_turn_x(1)
                pe_xT_there(pe, dense, 1, 1)
                features_turned(1)
                k_product(0)
                k_product(1)
                features((2, 3))
                for s in range(NT + 1):
                    if s < NT:
                        pe.wait_ge(a_exp, UNITS + s + 1)
                        turn_probs(("gat", s), probs[:, s % PROBS, :], s)
                    n = s - 1
                    if n >= 0:
                        for i in range(2):
                            k = turn.index[("gat", n, i)]
                            pe.wait_ge(turn_free[turn.owner[k]], turn.nth[k])
                        if n == 0:
                            pe.wait_ge(dense_free["dve"], dense.nth[dense.index[(1, "feat", 3)]])
                            pe.wait_ge(dense_free["act"], dense.nth[dense.index[(1, "k", 1)]])
                        if n >= 4:
                            pe.wait_ge(v_x, X_DONE[0] + n - 3)
                        for m in range(NT):
                            last = pe.matmul(bank_sc[:, gat_bank(n), 0:D], gat_pt[:, n % 2, m, :], v_sb[:, m, :],
                                             start=(m == 0), stop=(m == NT - 1))
                        last.then_inc(pe_pv, 1)

                def turn_normed(n, layer, h):
                    pe.wait_ge(v_normed, n * NT + 4 * (h + 1))
                    pe_turn_x(pe, dense, layer, normed, h)

                def down(pieces):
                    for i in pieces:
                        pe_rows_product(pe, dense, ("ffn", "down", i),
                                        lambda n, s, f: act_up[:, s, f, (2 * i + n) * P:(2 * i + n + 1) * P],
                                        lambda s, f: w_down[:, s, f, :], FC)

                turn_normed(0, 2, 0)
                pe.wait_ge(v_x, X_DONE[1])
                pe_xT_there(pe, dense, 2, 0)
                pe_qk(pe, dense, 1, (0, 1))
                turn_normed(0, 2, 1)
                pe_qk(pe, dense, 1, (2, 3))
                pe_xT_there(pe, dense, 2, 1)
                pe_qk(pe, dense, 1, range(4, 8))
                pe_v(pe, dense, 1)

                def up(pieces):
                    for i in pieces:
                        f, h = UP[i]
                        pe_xT_there(pe, dense, "ffn", h)
                        pe_product(pe, dense, ("ffn", "up", i), lambda s, c: w_up[:, s, c, f * P:(f + 1) * P],
                                   lambda s, c: xT[:, s, c, h * HALF:(h + 1) * HALF])

                attention(1, {HALF_FREE: lambda: turn_normed(1, "ffn", 0), PRODUCTS_DONE: lambda: up((0, 1)),
                              OUT_TURNED: lambda: up((2,)), PAIR_TURNED: lambda: up((3,))})
                up(range(4, XT_AT))
                turn_normed(1, "ffn", 1)
                pe.wait_ge(v_lo, dense.lo_done["ffn", "up", FC - 1])
                down((0,))
                up(range(XT_AT, 2 * FC))
                down((1,))
                pe.wait_ge(v_lo, dense.lo_done["ffn", "up", 2 * FC - 1])
                down((2,))

                pe.wait_ge(v_x, X_DONE[2] + 2)
                pe_turn_x(pe, dense, 3, x_sb, 0)
                down((3,))
                pe_xT_there(pe, dense, 3, 0)
                pe_qk(pe, dense, 2, (0, 1))
                pe.wait_ge(v_x, X_DONE[2] + 4)
                pe_turn_x(pe, dense, 3, x_sb, 1)
                pe_qk(pe, dense, 2, (2, 3))
                pe_xT_there(pe, dense, 3, 1)
                pe_qk(pe, dense, 2, range(4, 8))
                pe_v(pe, dense, 2)
                attention(2, {HALF_FREE: lambda: pe_layer0_turn_x(pe, in_loop),
                              PRODUCTS_DONE: lambda: pe_layer0_qk(pe, in_loop, (0, 1)),
                              OUT_TURNED: lambda: pe_layer0_qk(pe, in_loop, (2,)),
                              PAIR_TURNED: lambda: pe_layer0_qk(pe, in_loop, (3,))})
                pe_layer0_end(pe, in_loop)

            @block.scalar
            def _(act):
                def log(i):
                    tile = ring_adj[:, i % 4, :]
                    if i < NT:
                        if i >= 4:
                            act.wait_ge(adj_in[i % 4], 16 * (i // 4))
                        act.activation(tile, tile, ACT.Ln, bias=col("log_eps")).then_inc(a_ln, 1)
                    elif i < 3 * NT:
                        act.wait_ge(p_gate, 3 * (i - 2 * NT) + 2)
                        act.activation(col_row[:, :], col_row[:, :], ACT.Ln).then_inc(a_ln, 1)
                    else:
                        act.wait_ge(p_clip, i - 3 * NT + 1)
                        act.activation(tile, tile, ACT.Ln).then_inc(a_ln, 1)

                def take_turned(key, dst):
                    act.wait_ge(pe_turn, turn.filled(key))
                    act.activation(dst, bank_tr[:, turn.bank(key), :], ACT.Copy).then_inc(turn_free["act"], 1)

                def attention(a, meanwhile):
                    first = STACK[a] * NT
                    for s in range(LAST_STEP + 1):
                        u = s - LAG
                        if 0 <= u < UNITS:
                            group = u // 8
                            if u % 8 == 0 and group >= 2:
                                act.wait_ge(pe_pv, pvs_before[a] + group - 1)
                            if a == 0 and u == 14:
                                act.wait_ge(y_out, 16)
                            take_turned((a, "P", u, 0), pt[:, group % 2, u % 8, 0:4, :])
                        if s < UNITS:
                            act.wait_ge(v_low, v_low_before[a] + s + 1)
                            act.activation(probs[:, s % PROBS, :], probs[:, s % PROBS, :], ACT.Exp, scale=-1.0,
                                           bias=low_units[:, s % PROBS:s % PROBS + 1],
                                           accum_out=sums[:, s:s + 1]).then_inc(a_exp, 1)
                        if s % 16 in (6, 14) and s < 48:
                            log(first + 2 * (s // 16 + 1) + (s % 16 == 14))
                        if s >= 18 and (s - 18) % 8 == 0 and s < 8 * GROUPS + 18:
                            group = (s - 18) // 8
                            act.wait_ge(pe_pv, pvs_before[a] + group + 1)
                            if group >= 1:
                                act.wait_ge(pe_turn, turn.filled((a, "O", group - 1)))
                            act.activation(o_turned[:, :], bank_o[:, :], ACT.Copy).then_inc(a_o, 1)
                        if a and s >= 29 and (s - 29) % 16 == 0:
                            pair = (s - 29) // 16
                            if pair >= 1:
                                act.wait_ge(pe_turn, turn.filled((a, "W", pair - 1)))
                            take_turned((a, "T", pair), o_T[:, :, :].rearrange("p c n -> p (c n)"))
                        if s in meanwhile:
                            meanwhile[s]()

                act.preload_act_table_set("natural_log_exp_and_others")
                def take_featT(h):
                    for c in range(DC):
                        act_evacuate(act, dense, (1, "featT", c, h), featT[:, c, h * HALF:(h + 1) * HALF],
                                     ACT.Identity, bias=col("fcb", c))

                attention(0, {HALF_FREE: lambda: act_take_xT(act, dense, 1, 0), OUT_TURNED: lambda: take_featT(0)})

                def take_k(h):
                    act_evacuate(act, dense, (1, "k", h), col_row[:, h * HALF:(h + 1) * HALF], ACT.Identity,
                                 bias=col("kb"))

                act_take_xT(act, dense, 1, 1)
                take_featT(1)
                for h in range(2):
                    take_k(h)
                act.wait_ge(dense_free["act"], dense.nth[dense.index[(1, "k", 1)]])
                for s in range(NT + 2):
                    if s < NT:
                        act.wait_ge(v_rowadd, s // 4 + 1)
                        if s >= PROBS:
                            act.wait_ge(pe_turn, turn.filled(("gat", s - PROBS, 1)))
                        act.activation(probs[:, s % PROBS, :], col_row[:, :], ACT.Identity,
                                       bias=row_add[:, s:s + 1]).then_inc(a_line, 1)
                    n = s - 1
                    if 0 <= n < NT:
                        act.wait_ge(v_leaky, n + 1)
                        act.activation(probs[:, n % PROBS, :], probs[:, n % PROBS, :], ACT.Exp, scale=-1.0,
                                       bias=low2[:, n:n + 1], accum_out=sums[:, n:n + 1]).then_inc(a_exp, 1)
                    n = s - 2
                    if n >= 0:
                        if n >= 2:
                            act.wait_ge(pe_pv, GROUPS + n - 1)
                        take_turned(("gat", n, 0), gat_pt[:, n % 2, 0:4, :])

                act_take_xT(act, dense, 2, 0, "g1", "b1")
                act_take_qk(act, dense, 1, (0, 1))
                act_take_xT(act, dense, 2, 1, "g1", "b1")
                act_take_qk(act, dense, 1, range(2, 4))
                log(2 * NT)
                act_take_qk(act, dense, 1, range(4, 8))
                log(2 * NT + 1)

                def take_up(pieces):
                    for i in pieces:
                        f, h = UP[i]
                        act_split(act, dense, ("ffn", "up", i), act_up[:, 0, f, h * HALF:(h + 1) * HALF], ACT.Gelu,
                                  bias=col("bf1", f))

                attention(1, {HALF_FREE: lambda: act_take_xT(act, dense, "ffn", 0, "g2", "b2"),
                              PRODUCTS_DONE: lambda: take_up((0, 1)), OUT_TURNED: lambda: take_up((2,)),
                              PAIR_TURNED: lambda: take_up((3,))})
                take_up(range(4, XT_AT))
                act_take_xT(act, dense, "ffn", 1, "g2", "b2")
                take_up(range(XT_AT, 2 * FC))

                act.preload_act_table_set("natural_log_exp_and_others")
                act_take_xT(act, dense, 3, 0)
                act_take_qk(act, dense, 2, (0, 1))
                act_take_xT(act, dense, 3, 1)
                act_take_qk(act, dense, 2, range(2, 8))
                log(3 * NT)
                log(3 * NT + 1)
                attention(2, {HALF_FREE: lambda: act_layer0_xT(act, in_loop),
                              PRODUCTS_DONE: lambda: act_take_qk(act, dense, 0, (0, 1)),
                              OUT_TURNED: lambda: act_take_qk(act, dense, 0, (2,)),
                              PAIR_TURNED: lambda: act_take_qk(act, dense, 0, (3,))})
                act_layer0_end(act, in_loop)

            @block.vector
            def _(dve):
                own = Own(dve)
                link = own.link

                def biased(a, u):
                    p, g, n, h, tile = unit(u)
                    dve.wait_ge(pe_scores, a * UNITS + u + 1)
                    if g == 0 and u % 16 in (0, 4):
                        i = STACK[a] * NT + tile
                        if a == 2:
                            dve.wait_ge(a_ln, 2 * NT - 2 + tile + 1)
                        elif i >= 2:
                            dve.wait_ge(p_bias, i - 1)
                    if u >= PROBS:
                        dve.wait_ge(pe_turn, turn.filled((a, "P", u - PROBS, 1)))
                    dve.tensor_tensor_reduce(probs[:, u % PROBS, :], bank_sc[:, 2 * (u % 2):2 * (u % 2) + 2, :],
                                             ring_adj[:, tile % 4, :], -1.0, BIG, ALU.add, ALU.min,
                                             low_units[:, u % PROBS:u % PROBS + 1]).then_inc(v_low, 1)

                def finish(a, group):
                    g, p = group % 2, group // 2
                    of_group = slice(8 * group, 8 * group + 8)
                    if group >= 1:
                        dve.wait_ge(turn_free["dve"], turn.nth[turn.index[(a, "O", group - 1)]])
                    dve.wait_ge(a_exp, exps_before[a] + 8 * group + 8)
                    link(dve.reciprocal(recip, sums[:, of_group]))
                    key = (a, "O", group)
                    dve.wait_ge(pe_turn, turn.filled(key))
                    ins = dve.tensor_tensor(
                        o_nat[:, :, g * P:(g + 1) * P].rearrange("p n (j d) -> p n j d", j=HG),
                        bank_tr[:, turn.bank(key), 0:2 * P].rearrange("p (n j d) -> p n j d", n=2, j=HG),
                        recip.rearrange("p (n j) -> p n j", n=2).unsqueeze(3).to_broadcast([P, 2, HG, HD]), ALU.mult)
                    ins.then_inc(turn_free["dve"], 1)
                    if a == 0:
                        if group == 0:
                            dve.wait_ge(x_res_in, 16)
                        dve.wait_ge(turn_free["dve"], turn.nth[turn.index[key]])
                        xs = x_sb[:, 2 * p:2 * p + 2, g * P:(g + 1) * P]
                        dve.tensor_tensor(xs, xs, o_nat[:, :, g * P:(g + 1) * P], ALU.add).then_inc(v_x, 1)

                def project_out(a, pair):
                    key = (a, "W", pair)
                    xs = x_sb[:, 2 * pair:2 * pair + 2, :]
                    if pair:
                        row_stats(range(2 * pair - 2, 2 * pair))
                    link(dve.tensor_tensor(xs, xs, rows[:, R_BO[a]:R_BO[a] + 1, :].to_broadcast([P, 2, D]), ALU.add))
                    dve.wait_ge(pe_turn, turn.filled(key))
                    dve.tensor_tensor(xs, xs, bank_tr[:, turn.bank(key), :].rearrange("p (n d) -> p n d", n=2),
                                      ALU.add).then_inc(turn_free["dve"], 1)
                    dve.wait_ge(turn_free["dve"], turn.nth[turn.index[key]])
                    dve.sem_inc(v_x, 1)

                def take_turned(key, dst):
                    dve.wait_ge(pe_turn, turn.filled(key))
                    dve.tensor_copy(dst, bank_tr[:, turn.bank(key), :].rearrange("p (m n) -> p m n", n=P)
                                    ).then_inc(turn_free["dve"], 1)

                def attention(a, meanwhile):
                    for s in range(LAST_STEP + 1):
                        if s < UNITS:
                            biased(a, s)
                        u = s - LAG
                        if 0 <= u < UNITS:
                            group = u // 8
                            if u % 8 == 0 and group >= 2:
                                dve.wait_ge(pe_pv, pvs_before[a] + group - 1)
                            if a == 0 and u == 14:
                                dve.wait_ge(y_out, 16)
                            take_turned((a, "P", u, 1), pt[:, group % 2, u % 8, 4:8, :])
                        if a == 1 and s == HALF_FREE - 4:
                            variance(slice(0, 4))
                        if a == 1 and s == HALF_FREE:
                            dve.wait_ge(pe_pv, pvs_before[1] + GROUPS - 1)
                            normalise(1, 0)
                        if s >= 20 and (s - 20) % 8 == 0:
                            finish(a, (s - 20) // 8)
                        if a and s >= 30 and (s - 30) % 16 == 0:
                            project_out(a, (s - 30) // 16)
                        if s in meanwhile:
                            meanwhile[s]()

                def row_stats(tiles):
                    for i in tiles:
                        own.mark(dve.bn_stats(stats[:, i, :], x_sb[:, i, :]))
                    own.wait()
                    for i in tiles:
                        own.mark(dve.bn_aggr(mean_var[:, i, :], stats[:, i, :]))

                def variance(tiles):
                    own.wait()
                    dve.tensor_scalar(var_eps[:, tiles], mean_var[:, tiles, 1], LN_EPS, None, ALU.add
                                      ).then_inc(v_stats, 1)

                def normalise(n, h):
                    dve.wait_ge(p_rstd, 2 * n + h + 1)
                    for i in range(4 * h, 4 * h + 4):
                        dve.tensor_scalar(normed[:, i, :], x_sb[:, i, :], mean_var[:, i, 0:1], rstd[:, i:i + 1],
                                          ALU.subtract, ALU.mult).then_inc(v_normed, 1)

                def centre(tiles):
                    for i in tiles:
                        dve.scalar_tensor_tensor(out=y_sb[:, i, :], in0=x_sb[:, i, :], scalar=mean_var[:, i, 0:1],
                                                 in1=rows[:, R_GAMMA, :], op0=ALU.subtract, op1=ALU.mult
                                                 ).then_inc(v_centred, 1)

                def scale(tiles):
                    dve.wait_ge(p_rstd, 5)
                    dve.wait_ge(v_centred, tiles[-1] + 1)
                    for i in tiles:
                        dve.scalar_tensor_tensor(out=y_sb[:, i, :], in0=y_sb[:, i, :], scalar=rstd[:, i:i + 1],
                                                 in1=rows[:, R_BETA, :], op0=ALU.mult, op1=ALU.add
                                                 ).then_inc(v_normed, 1)

                def take_features(i):
                    dve_take_rows(dve, dense, (1, "feat", i), i, R_FCB)

                def q_rows(h):
                    dve.wait_ge(dense_free["dve"], dense.nth[dense.index[(1, "feat", 2 * h + 1)]])
                    dve_row_sums(dve, own, v_sb, R_QW, range(4 * h, 4 * h + 4), q_sums)
                    own.wait()
                    dve.tensor_scalar(row_add[:, 4 * h:4 * h + 4], q_sums[:, 4 * h:4 * h + 4], col("qb"), None,
                                      ALU.add).then_inc(v_rowadd, 1)

                attention(0, {HALF_FREE: lambda: dve_split_xT(dve, dense, 1, 0), PRODUCTS_DONE: lambda: take_features(0),
                              OUT_TURNED: lambda: take_features(1)})

                dve_split_xT(dve, dense, 1, 1)
                q_rows(0)
                for s in range(NT + 5):
                    if s < NT:
                        buf = probs[:, s % PROBS, :]
                        dve.wait_ge(a_line, s + 1)
                        dve.wait_ge(p_bias, NT + s - 1)
                        dve.tensor_tensor_reduce(buf, buf, ring_adj[:, s % 4, :], -1.0, BIG, ALU.add, ALU.min,
                                                 low[:, s:s + 1]).then_inc(v_low, 1)
                        dve.wait_ge(v_low, UNITS + s + 1)
                        link(dve.scalar_tensor_tensor(out=low2[:, s:s + 1], in0=low[:, s:s + 1], scalar=LEAK,
                                                      in1=low[:, s:s + 1], op0=ALU.mult, op1=ALU.min))
                        dve.scalar_tensor_tensor(out=buf, in0=buf, scalar=LEAK, in1=buf, op0=ALU.mult, op1=ALU.min
                                                 ).then_inc(v_leaky, 1)
                    if s == 1:
                        take_features(2)
                        take_features(3)
                    if s == 2:
                        q_rows(1)
                    n = s - 2
                    if 0 <= n < NT:
                        if n >= 2:
                            dve.wait_ge(pe_pv, GROUPS + n - 1)
                        take_turned(("gat", n, 1), gat_pt[:, n % 2, 4:8, :])
                    n = s - 4
                    if 0 <= n < NT:
                        dve.wait_ge(a_exp, UNITS + n + 1)
                        link(dve.reciprocal(recip[:, n:n + 1], sums[:, n:n + 1]))
                        dve.wait_ge(pe_pv, GROUPS + n + 1)
                        dve.scalar_tensor_tensor(out=x_sb[:, n, :], in0=bank_sc[:, gat_bank(n), 0:D],
                                                 scalar=recip[:, n:n + 1], in1=x_sb[:, n, :], op0=ALU.mult,
                                                 op1=ALU.add).then_inc(v_x, 1)
                    if 1 <= n <= NT:
                        dve.wait_ge(v_x, X_DONE[0] + n)
                        row_stats([n - 1])
                    if n == 4:
                        variance(slice(0, 4))
                    if n == 5:
                        normalise(0, 0)

                variance(slice(4, 8))
                dve_split_xT(dve, dense, 2, 0)
                normalise(0, 1)
                dve_split_qk(dve, dense, 1, (0, 1))
                dve_split_xT(dve, dense, 2, 1)
                dve_split_qk(dve, dense, 1, range(2, 8))
                for i in range(4):
                    dve_take_rows(dve, dense, (2, "v", i), i, R_BV[1])
                dve.wait_ge(v_normed, NT)

                def split_up(pieces):
                    for i in pieces:
                        f, h = UP[i]
                        dve_split(dve, dense, ("ffn", "up", i),
                                  *(act_up[:, s, f, h * HALF:(h + 1) * HALF] for s in range(2)))

                attention(1, {HALF_FREE: lambda: dve_split_xT(dve, dense, "ffn", 0), PRODUCTS_DONE: lambda: split_up((0, 1)),
                              OUT_TURNED: lambda: split_up((2,)), PAIR_TURNED: lambda: split_up((3,))})
                row_stats((NT - 2, NT - 1))
                variance(slice(4, 8))
                split_up(range(4, 6))
                normalise(1, 1)
                split_up(range(6, XT_AT))
                dve_split_xT(dve, dense, "ffn", 1)
                split_up((XT_AT,))

                def add_down(i):
                    xs = x_sb[:, 2 * i:2 * i + 2, :]
                    link(dve.tensor_tensor(xs, xs, rows[:, R_BF2:R_BF2 + 1, :].to_broadcast([P, 2, D]), ALU.add))
                    dve.wait_ge(pe_dense, dense.filled(("ffn", "down", i)))
                    dve.tensor_tensor(xs, xs, bank_sc[:, dense.bank(("ffn", "down", i)), :].rearrange(
                        "p (n d) -> p n d", n=2), ALU.add).then_inc(dense_free["dve"], 1)
                    dve.wait_ge(dense_free["dve"], dense.nth[dense.index[("ffn", "down", i)]])
                    dve.sem_inc(v_x, 1)

                dve.wait_ge(v_normed, 2 * NT)
                add_down(0)
                split_up(range(XT_AT + 1, 2 * FC))
                add_down(1)
                add_down(2)

                dve_split_xT(dve, dense, 3, 0)
                add_down(3)
                dve_split_qk(dve, dense, 2, (0, 1))
                dve_split_xT(dve, dense, 3, 1)
                dve_split_qk(dve, dense, 2, range(2, 8))
                for i in range(4):
                    dve_take_rows(dve, dense, (3, "v", i), i, R_BV[2])
                def split_and_centre(pieces, tiles):
                    dve_split_qk(dve, dense, 0, pieces)
                    centre(tiles)

                attention(2, {HALF_FREE: lambda: dve_layer0_start(dve, own, in_loop),
                              PRODUCTS_DONE: lambda: split_and_centre((0, 1), (0, 1)),
                              OUT_TURNED: lambda: split_and_centre((2,), (2, 3)),
                              PAIR_TURNED: lambda: dve_split_qk(dve, dense, 0, (3,))})
                row_stats((NT - 2, NT - 1))
                variance(slice(0, NT))
                dve_layer0_end(dve, in_loop, lambda k: scale((2 * k - 2, 2 * k - 1)) if k else centre(range(4, NT)))

        clear_semaphores()
    nc.sync.wait_ge(y_out, 16)
    nc.sync.wait_ge(x_res_in, 16)
    nc.sync.wait_ge(late_cat, 16 * STACK_DMAS)
    ctx.close()


INPUTS = ["x", "adj", "L0_gnn_W_q", "L0_gnn_b_q", "L0_gnn_W_k", "L0_gnn_b_k", "L0_gnn_W_v", "L0_gnn_b_v",
          "L0_gnn_w_g", "L0_gnn_b_g", "L1_gnn_fc_w", "L1_gnn_fc_b", "L1_gnn_q_w", "L1_gnn_q_b", "L1_gnn_k_w",
          "L1_gnn_k_b", "L2_gnn_Wq", "L2_gnn_bq", "L2_gnn_Wk", "L2_gnn_bk", "L2_gnn_Wv", "L2_gnn_bv", "L2_gnn_Wo",
          "L2_gnn_bo", "L2_gnn_g1", "L2_gnn_b1", "L2_gnn_g2", "L2_gnn_b2", "L2_gnn_Wf1", "L2_gnn_bf1", "L2_gnn_Wf2",
          "L2_gnn_bf2", "L3_gnn_Wq", "L3_gnn_bq", "L3_gnn_Wk", "L3_gnn_bk", "L3_gnn_Wv", "L3_gnn_bv", "L3_gnn_Wo",
          "L3_gnn_bo", "L3_gnn_gamma", "L3_gnn_beta"]


def kernel(**inputs):
    import numpy as _np
    import concourse.bacc as _bacc
    from concourse.bass_utils import run_bass_kernel_spmd as _run

    nc = _bacc.Bacc("TRN2", target_bir_lowering=False, num_devices=1)
    arrays, tensors = {}, {}
    for name in INPUTS:
        a = _np.ascontiguousarray(inputs[name])
        if a.ndim == 0:
            a = a.reshape(1)
        arrays[f"in_{name}"] = a
        tensors[name] = nc.dram_tensor(f"in_{name}", a.shape, mybir.dt.from_np(a.dtype), kind="ExternalInput").ap()
    tensors["out"] = nc.dram_tensor("out_0", (B, N, D), F32, kind="ExternalOutput").ap()
    graph_layers(nc, tensors)
    return _run(nc, [arrays], core_ids=[0]).results[0]["out_0"]
```
